# Optimizing a Trainium2 kernel written in Bass

```python
import numpy as np
import jax
import jax.numpy as jnp

def _softmax(x, axis=-1):
    return jax.nn.softmax(x, axis=axis)

def _gelu(x):
    return jax.nn.gelu(x, approximate=True)

def _silu(x):
    return jax.nn.silu(x)

def _sigmoid(x):
    return jax.nn.sigmoid(x)

def _layernorm(x, axis=-1, eps=1e-05):
    m = jnp.mean(x, axis=axis, keepdims=True)
    v = jnp.var(x, axis=axis, keepdims=True)
    return (x - m) / jnp.sqrt(v + eps)

def _scatter_add(tgt, idx, src, axis=0):
    return tgt.at[idx].add(src)

def _segment_sum(src, seg, n):
    return jax.ops.segment_sum(src, seg, n)
kernel_name = 'mk_flamingo_gated_d4_seqx_r4_48f84c'

def setup_inputs(seed: int=0):
    np.random.seed(seed)
    _w = jnp.asarray

    def _rec_inputs():
        import jax
        import jax.numpy as jnp
        _rk = jax.random.key(seed)
        x = -0.0002928 + 1 * jax.random.normal(jax.random.fold_in(_rk, 1), (8, 256, 512), jnp.float32)
        _lenS = 256 - jax.random.randint(jax.random.fold_in(_rk, 7), (8,), 0, max(1, 256 // 4) + 1, jnp.int32)
        _lenS2 = 256 - jax.random.randint(jax.random.fold_in(_rk, 8), (8,), 0, max(1, 256 // 4) + 1, jnp.int32)
        fside_S2_0 = -0.00337071 + 1.01897 * jax.random.normal(jax.random.fold_in(_rk, 11), (256,), jnp.float32)
        _ctx_2048P = jax.random.normal(jax.random.fold_in(_rk, 12), (8, 16, 512), jnp.float32)
        _ctx_2048c = jax.random.dirichlet(jax.random.fold_in(_rk, 512), 0.3 * jnp.ones((16,), jnp.float32), (8, 256))
        _ctx_2048t = jnp.einsum('bsk,bkd->bsd', _ctx_2048c, _ctx_2048P)
        _ctx_2048t = _ctx_2048t * jax.lax.rsqrt(jnp.mean(jnp.square(_ctx_2048t)) + 1e-12) * 0.953939
        ctx_2048 = 0.000675642 + 1.00031 * (_ctx_2048t + 0.3 * jax.random.normal(jax.random.fold_in(_rk, 612), (8, 256, 512), jnp.float32))
        _validS = jnp.arange(256)[None, :] < _lenS[:, None]
        _validS2 = jnp.arange(256)[None, :] < _lenS2[:, None]
        _causal = jnp.tril(jnp.ones((256, 256), dtype=bool))
        mask_SxS2_bc0 = jnp.logical_not(jnp.broadcast_to(_validS2[0:1, :], (256, 256)))
        mask_BxS2_bk0 = jnp.logical_not(jnp.broadcast_to(_validS2[:, :], (8, 256)))
        _g = jax.random.normal(jax.random.fold_in(_rk, 9001), (2, 4), jnp.float32)
        _g = jnp.sign(_g) * jnp.maximum(jnp.abs(_g), 1.0) + (_g == 0) * 1.0
        g_xattn = _g[0]
        g_ffn = _g[1]
        return (x, fside_S2_0, ctx_2048, mask_SxS2_bc0, mask_BxS2_bk0, g_xattn, g_ffn)
    x, fside_S2_0, ctx_2048, mask_SxS2_bc0, mask_BxS2_bk0, g_xattn, g_ffn = _rec_inputs()

    def _L0_xattn_setup():
        import jax, jax.numpy as jnp
        import numpy as np
        key = jax.random.key(seed)
        ks = jax.random.split(key, 5)
        B, D, L, NH = (2, 256, 512, 8)
        H = D // NH
        return {'v': jax.random.normal(ks[0], (B, D, L), jnp.float32), 'k': jax.random.normal(ks[1], (H, L), jnp.float32) * 0.1, 'bias': jax.random.normal(ks[2], (D,), jnp.float32), 'x1': jax.random.normal(ks[3], (B, D, L), jnp.float32), 'x2': jax.random.normal(ks[4], (B, D, L), jnp.float32), 'num_heads': NH}
    _L0_xattn_all = _L0_xattn_setup()
    _L0_xattn_in = {k: v for k, v in _L0_xattn_all.items() if k in ('k',)}
    del _L0_xattn_all

    def _L0_ffn_setup():
        import jax, jax.numpy as jnp
        import numpy as np
        D_MODEL = 512
        D_EXPERT = 2048
        EPS = 1e-08

        def ternary_quant(w):
            scale = jnp.mean(jnp.abs(w)) + EPS
            q = jnp.clip(jnp.round(w / scale), -1.0, 1.0) * scale
            return w + jax.lax.stop_gradient(q - w)
        key = jax.random.key(seed)
        k_x, k_up, k_gate, k_down = jax.random.split(key, 4)
        std_in = 1.0 / np.sqrt(D_MODEL)
        std_exp = 1.0 / np.sqrt(D_EXPERT)
        return {'x': jax.random.normal(k_x, (4, 512, D_MODEL), dtype=jnp.float32), 'W_up': jax.random.normal(k_up, (D_EXPERT, D_MODEL), dtype=jnp.float32) * std_in, 'W_gate': jax.random.normal(k_gate, (D_EXPERT, D_MODEL), dtype=jnp.float32) * std_in, 'W_down': jax.random.normal(k_down, (D_MODEL, D_EXPERT), dtype=jnp.float32) * std_exp}
    _L0_ffn_all = _L0_ffn_setup()
    _L0_ffn_in = {k: v for k, v in _L0_ffn_all.items() if k in ('W_up', 'W_gate', 'W_down')}
    del _L0_ffn_all

    def _L1_xattn_setup():
        import jax, jax.numpy as jnp
        import numpy as np
        B_DIM, T_DIM, C_DIM = (16, 256, 512)

        def _wkv(w, u, k, v):
            Bn, Tn, Cn = k.shape
            NEG_INF = jnp.float32(-1e+38)

            def step(carry, kv_t):
                p, q, o = carry
                kt, vt = kv_t
                no = jnp.maximum(o, u + kt)
                A = jnp.exp(o - no)
                E = jnp.exp(u + kt - no)
                y = (A * p + E * vt) / (A * q + E)
                no2 = jnp.maximum(w + o, kt)
                A2 = jnp.exp(w + o - no2)
                E2 = jnp.exp(kt - no2)
                return ((A2 * p + E2 * vt, A2 * q + E2, no2), y)
            init = (jnp.zeros((Bn, Cn), k.dtype), jnp.zeros((Bn, Cn), k.dtype), jnp.full((Bn, Cn), NEG_INF, k.dtype))
            kT = jnp.moveaxis(k, 1, 0)
            vT = jnp.moveaxis(v, 1, 0)
            _, yT = jax.lax.scan(step, init, (kT, vT))
            return jnp.moveaxis(yT, 0, 1)
        key = jax.random.key(seed)
        k1, k2, k3, k4 = jax.random.split(key, 4)
        w = -jnp.exp(jax.random.normal(k1, (C_DIM,), jnp.float32))
        u = jax.random.normal(k2, (C_DIM,), jnp.float32)
        k = jax.random.normal(k3, (B_DIM, T_DIM, C_DIM), jnp.float32)
        v = jax.random.normal(k4, (B_DIM, T_DIM, C_DIM), jnp.float32)
        return {'B': B_DIM, 'T': T_DIM, 'C': C_DIM, 'w': w, 'u': u, 'k': k, 'v': v}
    _L1_xattn_all = _L1_xattn_setup()
    _L1_xattn_in = {k: v for k, v in _L1_xattn_all.items() if k in ('w', 'u')}
    del _L1_xattn_all

    def _L1_ffn_setup():
        import jax, jax.numpy as jnp
        import numpy as np
        key = jax.random.key(seed)
        k1, k2, k3, k4 = jax.random.split(key, 4)
        B, S, D_IN, D_OUT = (4, 1024, 512, 512)
        x = jax.random.normal(k1, (B, S, D_IN), dtype=jnp.float32)
        weight = jax.random.normal(k2, (D_OUT, D_IN), dtype=jnp.float32) * 0.02
        scale_weight = jax.random.uniform(k3, (D_OUT,), dtype=jnp.float32, minval=0.5, maxval=1.5)
        bias = jax.random.normal(k4, (D_OUT,), dtype=jnp.float32) * 0.02
        return {'x': x, 'weight': weight, 'scale_weight': scale_weight, 'bias': bias}
    _L1_ffn_all = _L1_ffn_setup()
    _L1_ffn_in = {k: v for k, v in _L1_ffn_all.items() if k in ('weight', 'scale_weight', 'bias')}
    del _L1_ffn_all

    def _L2_xattn_setup():
        import jax, jax.numpy as jnp
        import numpy as np
        B, LQ, LKV = (4, 256, 256)
        HID, H, G = (512, 32, 8)
        HD = HID // H
        HPG = H // G
        key = jax.random.key(seed)
        ks = jax.random.split(key, 10)
        s = 0.02
        inp = {'X': jax.random.normal(ks[0], (B, LQ, HID), jnp.float32), 'encoder_output': jax.random.normal(ks[1], (B, LKV, HID), jnp.float32), 'causal_mask': jnp.triu(jnp.ones((LQ, LKV), bool), 1), 'padding_mask': jnp.zeros((B, LKV), bool).at[B // 2:, LKV - LKV // 4:].set(True), 'Wq': jax.random.normal(ks[2], (HID, HID), jnp.float32) * s, 'bq': jnp.zeros((HID,), jnp.float32), 'Wk': jax.random.normal(ks[3], (G * HD, HID), jnp.float32) * s, 'bk': jnp.zeros((G * HD,), jnp.float32), 'Wv': jax.random.normal(ks[4], (G * HD, HID), jnp.float32) * s, 'bv': jnp.zeros((G * HD,), jnp.float32), 'Wo': jax.random.normal(ks[5], (HID, HID), jnp.float32) * s, 'bo': jnp.zeros((HID,), jnp.float32)}
        return inp
    _L2_xattn_all = _L2_xattn_setup()
    _L2_xattn_in = {k: v for k, v in _L2_xattn_all.items() if k in ('Wq', 'bq', 'Wk', 'bk', 'Wv', 'bv', 'Wo', 'bo')}
    del _L2_xattn_all

    def _L2_ffn_setup():
        import jax, jax.numpy as jnp
        import numpy as np
        TARGET_SPARSITY = 0.9
        LN_EPS = 1e-05

        def ternary_quant(W):
            scale = jnp.mean(jnp.abs(W))
            q = jnp.clip(jnp.round(W / (scale + 1e-08)), -1.0, 1.0) * scale
            return W + jax.lax.stop_gradient(q - W)

        def layernorm(x, gamma, beta):
            mu = jnp.mean(x, axis=-1, keepdims=True)
            var = jnp.var(x, axis=-1, keepdims=True)
            return (x - mu) * jax.lax.rsqrt(var + LN_EPS) * gamma + beta
        key = jax.random.key(seed)
        ks = jax.random.split(key, 3)
        B, S, D, N = (4, 512, 512, 2048)
        x = jax.random.normal(ks[0], (B, S, D), dtype=jnp.float32)
        W_syn = jax.random.normal(ks[1], (N, D), dtype=jnp.float32) * (1.0 / np.sqrt(D))
        b_syn = jnp.zeros((N,), dtype=jnp.float32)
        W_out = jax.random.normal(ks[2], (D, N), dtype=jnp.float32) * (1.0 / np.sqrt(N))
        b_out = jnp.zeros((D,), dtype=jnp.float32)
        gamma = jnp.ones((D,), dtype=jnp.float32)
        beta = jnp.zeros((D,), dtype=jnp.float32)
        return {'x': x, 'W_syn': W_syn, 'b_syn': b_syn, 'W_out': W_out, 'b_out': b_out, 'gamma': gamma, 'beta': beta}
    _L2_ffn_all = _L2_ffn_setup()
    _L2_ffn_in = {k: v for k, v in _L2_ffn_all.items() if k in ('W_syn', 'b_syn', 'W_out', 'b_out', 'gamma', 'beta')}
    del _L2_ffn_all

    def _L3_xattn_setup():
        import jax, jax.numpy as jnp
        import numpy as np
        HIDDEN = 512
        NUM_HEADS = 16
        NUM_KV_HEADS = 4
        HEAD_DIM = 128
        ROPE_THETA = 10000.0
        EPS = 1e-06

        def rms_norm(x, w, eps=EPS):
            var = jnp.mean(jnp.square(x), axis=-1, keepdims=True)
            return x * jax.lax.rsqrt(var + eps) * w

        def rope_cache(L, head_dim, theta, dtype):
            inv_freq = 1.0 / theta ** (jnp.arange(0, head_dim, 2, dtype=jnp.float32) / head_dim)
            t = jnp.arange(L, dtype=jnp.float32)
            freqs = jnp.outer(t, inv_freq)
            emb = jnp.concatenate([freqs, freqs], -1)
            cos = jnp.cos(emb).astype(dtype)[None, :, None, :]
            sin = jnp.sin(emb).astype(dtype)[None, :, None, :]
            return (cos, sin)

        def rotate_half(x):
            x1, x2 = jnp.split(x, 2, axis=-1)
            return jnp.concatenate([-x2, x1], axis=-1)
        key = jax.random.key(seed)
        ks = jax.random.split(key, 10)
        B, L, T = (2, 512, 128)
        q_out = NUM_HEADS * HEAD_DIM
        kv_out = NUM_KV_HEADS * HEAD_DIM
        s = lambda fan_in: 1.0 / np.sqrt(fan_in)
        return {'x': jax.random.normal(ks[0], (B, L, HIDDEN), jnp.float32), 'h_ctx_kv': jax.random.normal(ks[1], (B, T, HIDDEN), jnp.float32), 'wq': jax.random.normal(ks[2], (HIDDEN, q_out), jnp.float32) * s(HIDDEN), 'wk': jax.random.normal(ks[3], (HIDDEN, kv_out), jnp.float32) * s(HIDDEN), 'wv': jax.random.normal(ks[4], (HIDDEN, kv_out), jnp.float32) * s(HIDDEN), 'wo': jax.random.normal(ks[5], (q_out, HIDDEN), jnp.float32) * s(q_out), 'wk_ctx': jax.random.normal(ks[6], (HIDDEN, kv_out), jnp.float32) * s(HIDDEN), 'wv_ctx': jax.random.normal(ks[7], (HIDDEN, kv_out), jnp.float32) * s(HIDDEN), 'q_norm_w': jnp.ones((HEAD_DIM,), jnp.float32), 'k_norm_w': jnp.ones((HEAD_DIM,), jnp.float32)}
    _L3_xattn_all = _L3_xattn_setup()
    _L3_xattn_in = {k: v for k, v in _L3_xattn_all.items() if k in ('wq', 'wk', 'wv', 'wo', 'wk_ctx', 'wv_ctx', 'q_norm_w', 'k_norm_w')}
    del _L3_xattn_all

    def _L3_ffn_setup():
        import jax, jax.numpy as jnp
        import numpy as np

        @jax.custom_vjp
        def ste_sign(x):
            return jnp.sign(x)

        def _ste_fwd(x):
            return (jnp.sign(x), None)

        def _ste_bwd(_, g):
            return (g,)
        ste_sign.defvjp(_ste_fwd, _ste_bwd)
        D_MODEL = 512
        D_HIDDEN = 2048
        key = jax.random.key(seed)
        k_x, k_up, k_dn = jax.random.split(key, 3)
        x = jax.random.normal(k_x, (2, 512, D_MODEL), dtype=jnp.float32)
        up_weight = jax.random.normal(k_up, (D_HIDDEN, D_MODEL), dtype=jnp.float32) * 0.02
        down_weight = jax.random.normal(k_dn, (D_MODEL, D_HIDDEN), dtype=jnp.float32) * 0.02
        up_scale = jnp.ones((D_HIDDEN,), dtype=jnp.float32)
        down_scale = jnp.ones((D_MODEL,), dtype=jnp.float32)
        output_scale = jnp.ones((1,), dtype=jnp.float32)
        return {'x': x, 'up_weight': up_weight, 'down_weight': down_weight, 'up_scale': up_scale, 'down_scale': down_scale, 'output_scale': output_scale}
    _L3_ffn_all = _L3_ffn_setup()
    _L3_ffn_in = {k: v for k, v in _L3_ffn_all.items() if k in ('up_weight', 'down_weight', 'up_scale', 'down_scale', 'output_scale')}
    del _L3_ffn_all
    return {'x': x, 'fside_S2_0': fside_S2_0, 'ctx_2048': ctx_2048, 'mask_SxS2_bc0': mask_SxS2_bc0, 'mask_BxS2_bk0': mask_BxS2_bk0, 'g_xattn': g_xattn, 'g_ffn': g_ffn, 'L0_xattn_k': _L0_xattn_in['k'], 'L0_ffn_W_up': _L0_ffn_in['W_up'], 'L0_ffn_W_gate': _L0_ffn_in['W_gate'], 'L0_ffn_W_down': _L0_ffn_in['W_down'], 'L1_xattn_w': _L1_xattn_in['w'], 'L1_xattn_u': _L1_xattn_in['u'], 'L1_ffn_weight': _L1_ffn_in['weight'], 'L1_ffn_scale_weight': _L1_ffn_in['scale_weight'], 'L1_ffn_bias': _L1_ffn_in['bias'], 'L2_xattn_Wq': _L2_xattn_in['Wq'], 'L2_xattn_bq': _L2_xattn_in['bq'], 'L2_xattn_Wk': _L2_xattn_in['Wk'], 'L2_xattn_bk': _L2_xattn_in['bk'], 'L2_xattn_Wv': _L2_xattn_in['Wv'], 'L2_xattn_bv': _L2_xattn_in['bv'], 'L2_xattn_Wo': _L2_xattn_in['Wo'], 'L2_xattn_bo': _L2_xattn_in['bo'], 'L2_ffn_W_syn': _L2_ffn_in['W_syn'], 'L2_ffn_b_syn': _L2_ffn_in['b_syn'], 'L2_ffn_W_out': _L2_ffn_in['W_out'], 'L2_ffn_b_out': _L2_ffn_in['b_out'], 'L2_ffn_gamma': _L2_ffn_in['gamma'], 'L2_ffn_beta': _L2_ffn_in['beta'], 'L3_xattn_wq': _L3_xattn_in['wq'], 'L3_xattn_wk': _L3_xattn_in['wk'], 'L3_xattn_wv': _L3_xattn_in['wv'], 'L3_xattn_wo': _L3_xattn_in['wo'], 'L3_xattn_wk_ctx': _L3_xattn_in['wk_ctx'], 'L3_xattn_wv_ctx': _L3_xattn_in['wv_ctx'], 'L3_xattn_q_norm_w': _L3_xattn_in['q_norm_w'], 'L3_xattn_k_norm_w': _L3_xattn_in['k_norm_w'], 'L3_ffn_up_weight': _L3_ffn_in['up_weight'], 'L3_ffn_down_weight': _L3_ffn_in['down_weight'], 'L3_ffn_up_scale': _L3_ffn_in['up_scale'], 'L3_ffn_down_scale': _L3_ffn_in['down_scale'], 'L3_ffn_output_scale': _L3_ffn_in['output_scale']}

def reference(x, fside_S2_0, ctx_2048, mask_SxS2_bc0, mask_BxS2_bk0, g_xattn, g_ffn, L0_xattn_k, L0_ffn_W_up, L0_ffn_W_gate, L0_ffn_W_down, L1_xattn_w, L1_xattn_u, L1_ffn_weight, L1_ffn_scale_weight, L1_ffn_bias, L2_xattn_Wq, L2_xattn_bq, L2_xattn_Wk, L2_xattn_bk, L2_xattn_Wv, L2_xattn_bv, L2_xattn_Wo, L2_xattn_bo, L2_ffn_W_syn, L2_ffn_b_syn, L2_ffn_W_out, L2_ffn_b_out, L2_ffn_gamma, L2_ffn_beta, L3_xattn_wq, L3_xattn_wk, L3_xattn_wv, L3_xattn_wo, L3_xattn_wk_ctx, L3_xattn_wv_ctx, L3_xattn_q_norm_w, L3_xattn_k_norm_w, L3_ffn_up_weight, L3_ffn_down_weight, L3_ffn_up_scale, L3_ffn_down_scale, L3_ffn_output_scale):
    import jax
    import jax.numpy as jnp

    def _L0_xattn_ref(v, k, bias, x1, x2, num_heads):
        import jax, jax.numpy as jnp
        import numpy as np
        B, D, L = v.shape
        H = D // num_heads
        fft_size = 2 * L
        vr = v.reshape(B, H, num_heads, L)
        x1r = x1.reshape(B, H, num_heads, L)
        x2r = x2.reshape(B, H, num_heads, L)
        kv = vr[:, :, :, None, :] * x2r[:, :, None, :, :]
        k_f = jnp.fft.rfft(k.astype(jnp.float32), n=fft_size)
        y = jnp.fft.irfft(jnp.fft.rfft(kv, n=fft_size) * k_f[None, :, None, None, :], n=fft_size)[..., :L]
        skip = bias.astype(jnp.float32).reshape(H, num_heads)[None, :, :, None, None]
        y = y + kv * skip
        out = jnp.einsum('bhijl,bhil->bhjl', y, x1r)
        return out.reshape(B, D, L)

    def _L0_ffn_ref(x, W_up, W_gate, W_down):
        import jax, jax.numpy as jnp
        import numpy as np
        D_MODEL = 512
        D_EXPERT = 2048
        EPS = 1e-08

        def ternary_quant(w):
            scale = jnp.mean(jnp.abs(w)) + EPS
            q = jnp.clip(jnp.round(w / scale), -1.0, 1.0) * scale
            return w + jax.lax.stop_gradient(q - w)
        wu = ternary_quant(W_up)
        wg = ternary_quant(W_gate)
        wd = ternary_quant(W_down)
        up = jnp.einsum('bsd,ed->bse', x, wu)
        gate = jnp.einsum('bsd,ed->bse', x, wg)
        hidden = jax.nn.silu(up) * gate
        return jnp.einsum('bse,de->bsd', hidden, wd)

    def _L1_xattn_ref(B, T, C, w, u, k, v):
        import jax, jax.numpy as jnp
        import numpy as np
        B_DIM, T_DIM, C_DIM = (16, 256, 512)

        def _wkv(w, u, k, v):
            Bn, Tn, Cn = k.shape
            NEG_INF = jnp.float32(-1e+38)

            def step(carry, kv_t):
                p, q, o = carry
                kt, vt = kv_t
                no = jnp.maximum(o, u + kt)
                A = jnp.exp(o - no)
                E = jnp.exp(u + kt - no)
                y = (A * p + E * vt) / (A * q + E)
                no2 = jnp.maximum(w + o, kt)
                A2 = jnp.exp(w + o - no2)
                E2 = jnp.exp(kt - no2)
                return ((A2 * p + E2 * vt, A2 * q + E2, no2), y)
            init = (jnp.zeros((Bn, Cn), k.dtype), jnp.zeros((Bn, Cn), k.dtype), jnp.full((Bn, Cn), NEG_INF, k.dtype))
            kT = jnp.moveaxis(k, 1, 0)
            vT = jnp.moveaxis(v, 1, 0)
            _, yT = jax.lax.scan(step, init, (kT, vT))
            return jnp.moveaxis(yT, 0, 1)
        return _wkv(w, u, k, v)

    def _L1_ffn_ref(x, weight, scale_weight, bias):
        import jax, jax.numpy as jnp
        import numpy as np
        w = weight * scale_weight[:, None]
        out = jnp.einsum('bsi,oi->bso', x, w) + bias
        return out

    def _L2_xattn_ref(X, encoder_output, causal_mask, padding_mask, Wq, bq, Wk, bk, Wv, bv, Wo, bo):
        import jax, jax.numpy as jnp
        import numpy as np
        B, LQ, LKV = (4, 256, 256)
        HID, H, G = (512, 32, 8)
        HD = HID // H
        HPG = H // G
        b = X.shape[0]
        q = X @ Wq.T + bq
        k = encoder_output @ Wk.T + bk
        v = encoder_output @ Wv.T + bv
        q = q.reshape(b, LQ, G, HPG, HD).transpose(0, 2, 3, 1, 4)
        k = k.reshape(b, LKV, G, HD).transpose(0, 2, 1, 3)
        v = v.reshape(b, LKV, G, HD).transpose(0, 2, 1, 3)
        scores = jnp.einsum('bgrqd,bgkd->bgrqk', q, k) / jnp.sqrt(jnp.float32(HD))
        scores = jnp.where(causal_mask[None, None, None, :, :], -jnp.inf, scores)
        scores = jnp.where(padding_mask[:, None, None, None, :], -jnp.inf, scores)
        w = jax.nn.softmax(scores, axis=-1)
        out = jnp.einsum('bgrqk,bgkd->bgrqd', w, v)
        out = out.reshape(b, H, LQ, HD).transpose(0, 2, 1, 3).reshape(b, LQ, HID)
        return out @ Wo.T + bo

    def _L2_ffn_ref(x, W_syn, b_syn, W_out, b_out, gamma, beta):
        import jax, jax.numpy as jnp
        import numpy as np
        TARGET_SPARSITY = 0.9
        LN_EPS = 1e-05

        def ternary_quant(W):
            scale = jnp.mean(jnp.abs(W))
            q = jnp.clip(jnp.round(W / (scale + 1e-08)), -1.0, 1.0) * scale
            return W + jax.lax.stop_gradient(q - W)

        def layernorm(x, gamma, beta):
            mu = jnp.mean(x, axis=-1, keepdims=True)
            var = jnp.var(x, axis=-1, keepdims=True)
            return (x - mu) * jax.lax.rsqrt(var + LN_EPS) * gamma + beta
        B, S, D = x.shape
        N = W_syn.shape[0]
        x_flat = x.reshape(-1, D)
        z = x_flat @ ternary_quant(W_syn).T + b_syn
        k = max(1, int(N * (1.0 - TARGET_SPARSITY)))
        topv, _ = jax.lax.top_k(z, k)
        thresh = topv[:, -1:]
        hidden = jnp.where(z >= thresh, jax.nn.relu(z), 0.0)
        out = hidden @ ternary_quant(W_out).T + b_out
        out = out.reshape(B, S, D)
        return layernorm(x + out, gamma, beta)

    def _L3_xattn_ref(x, h_ctx_kv, wq, wk, wv, wo, wk_ctx, wv_ctx, q_norm_w, k_norm_w):
        import jax, jax.numpy as jnp
        import numpy as np
        HIDDEN = 512
        NUM_HEADS = 16
        NUM_KV_HEADS = 4
        HEAD_DIM = 128
        ROPE_THETA = 10000.0
        EPS = 1e-06

        def rms_norm(x, w, eps=EPS):
            var = jnp.mean(jnp.square(x), axis=-1, keepdims=True)
            return x * jax.lax.rsqrt(var + eps) * w

        def rope_cache(L, head_dim, theta, dtype):
            inv_freq = 1.0 / theta ** (jnp.arange(0, head_dim, 2, dtype=jnp.float32) / head_dim)
            t = jnp.arange(L, dtype=jnp.float32)
            freqs = jnp.outer(t, inv_freq)
            emb = jnp.concatenate([freqs, freqs], -1)
            cos = jnp.cos(emb).astype(dtype)[None, :, None, :]
            sin = jnp.sin(emb).astype(dtype)[None, :, None, :]
            return (cos, sin)

        def rotate_half(x):
            x1, x2 = jnp.split(x, 2, axis=-1)
            return jnp.concatenate([-x2, x1], axis=-1)
        B, L, _ = x.shape
        T = h_ctx_kv.shape[1]
        rep = NUM_HEADS // NUM_KV_HEADS
        q = (x @ wq).reshape(B, L, NUM_HEADS, HEAD_DIM)
        k = (x @ wk).reshape(B, L, NUM_KV_HEADS, HEAD_DIM)
        v = (x @ wv).reshape(B, L, NUM_KV_HEADS, HEAD_DIM)
        q = rms_norm(q, q_norm_w)
        k = rms_norm(k, k_norm_w)
        k_ctx = (h_ctx_kv @ wk_ctx).reshape(B, T, NUM_KV_HEADS, HEAD_DIM)
        v_ctx = (h_ctx_kv @ wv_ctx).reshape(B, T, NUM_KV_HEADS, HEAD_DIM)
        k_ctx = rms_norm(k_ctx, k_norm_w)
        cos, sin = rope_cache(L, HEAD_DIM, ROPE_THETA, x.dtype)
        q = q * cos + rotate_half(q) * sin
        k = k * cos + rotate_half(k) * sin
        k_full = jnp.concatenate([k_ctx, k], axis=1)
        v_full = jnp.concatenate([v_ctx, v], axis=1)
        k_full = jnp.repeat(k_full, rep, axis=2)
        v_full = jnpp_repeat = jnp.repeat(v_full, rep, axis=2)
        i = jnp.arange(L)[:, None]
        j = jnp.arange(L)[None, :]
        causal = jnp.where(j > i, -jnp.inf, 0.0).astype(x.dtype)
        mask = jnp.concatenate([jnp.zeros((L, T), x.dtype), causal], axis=1)
        scale = 1.0 / np.sqrt(HEAD_DIM)
        scores = jnp.einsum('blhd,bmhd->bhlm', q, k_full) * scale + mask
        probs = jax.nn.softmax(scores, axis=-1)
        out = jnp.einsum('bhlm,bmhd->blhd', probs, v_full)
        out = out.reshape(B, L, NUM_HEADS * HEAD_DIM)
        return out @ wo

    def _L3_ffn_ref(x, up_weight, down_weight, up_scale, down_scale, output_scale):
        import jax, jax.numpy as jnp
        import numpy as np

        @jax.custom_vjp
        def ste_sign(x):
            return jnp.sign(x)

        def _ste_fwd(x):
            return (jnp.sign(x), None)

        def _ste_bwd(_, g):
            return (g,)
        ste_sign.defvjp(_ste_fwd, _ste_bwd)
        D_MODEL = 512
        D_HIDDEN = 2048
        up_w = ste_sign(up_weight)
        down_w = ste_sign(down_weight)
        hidden = jnp.einsum('bsd,hd->bsh', x, up_w) * up_scale
        hidden = jax.nn.relu(hidden)
        out = jnp.einsum('bsh,dh->bsd', hidden, down_w) * down_scale
        return out * output_scale
    x = x + jnp.tanh(g_xattn[0]) * _L0_xattn_ref(_layernorm(x, axis=-1), L0_xattn_k, fside_S2_0, ctx_2048, ctx_2048, 8)
    x = x + jnp.tanh(g_ffn[0]) * _L0_ffn_ref(_layernorm(x, axis=-1), L0_ffn_W_up, L0_ffn_W_gate, L0_ffn_W_down)
    x = x + jnp.tanh(g_xattn[1]) * _L1_xattn_ref(8, 256, 512, L1_xattn_w, L1_xattn_u, _layernorm(x, axis=-1), ctx_2048)
    x = x + jnp.tanh(g_ffn[1]) * _L1_ffn_ref(_layernorm(x, axis=-1), L1_ffn_weight, L1_ffn_scale_weight, L1_ffn_bias)
    x = x + jnp.tanh(g_xattn[2]) * _L2_xattn_ref(_layernorm(x, axis=-1), ctx_2048, mask_SxS2_bc0, mask_BxS2_bk0, L2_xattn_Wq, L2_xattn_bq, L2_xattn_Wk, L2_xattn_bk, L2_xattn_Wv, L2_xattn_bv, L2_xattn_Wo, L2_xattn_bo)
    x = x + jnp.tanh(g_ffn[2]) * _L2_ffn_ref(_layernorm(x, axis=-1), L2_ffn_W_syn, L2_ffn_b_syn, L2_ffn_W_out, L2_ffn_b_out, L2_ffn_gamma, L2_ffn_beta)
    x = x + jnp.tanh(g_xattn[3]) * _L3_xattn_ref(_layernorm(x, axis=-1), ctx_2048, L3_xattn_wq, L3_xattn_wk, L3_xattn_wv, L3_xattn_wo, L3_xattn_wk_ctx, L3_xattn_wv_ctx, L3_xattn_q_norm_w, L3_xattn_k_norm_w)
    x = x + jnp.tanh(g_ffn[3]) * _L3_ffn_ref(_layernorm(x, axis=-1), L3_ffn_up_weight, L3_ffn_down_weight, L3_ffn_up_scale, L3_ffn_down_scale, L3_ffn_output_scale)
    return x

_drawn_inputs = setup_inputs


def setup_inputs(seed=0):
    import zlib

    import numpy as np

    out = dict(_drawn_inputs(seed))
    spreads = {'L2_xattn_bq': (0.0, 0.8),
     'L2_xattn_bk': (0.0, 0.8),
     'L2_xattn_bv': (0.0, 0.8),
     'L2_xattn_bo': (0.0, 0.42),
     'L2_ffn_b_syn': (0.0, 0.406),
     'L2_ffn_b_out': (0.0, 0.368),
     'L2_ffn_gamma': (1.0, 0.2),
     'L2_ffn_beta': (0.0, 0.36),
     'L3_xattn_q_norm_w': (1.0, 0.6),
     'L3_xattn_k_norm_w': (1.0, 0.6),
     'L3_ffn_up_scale': (1.0, 0.2),
     'L3_ffn_down_scale': (1.0, 0.2)}
    factors = {'L1_ffn_bias': 8.0,
     'L2_xattn_Wq': 8.0,
     'L2_xattn_Wk': 8.0,
     'L2_xattn_Wv': 2.722,
     'L3_xattn_wk': 4.259,
     'L3_xattn_wv': 2.765}
    for name, (base, spread) in spreads.items():
        noise = np.random.default_rng([zlib.crc32(name.encode()), seed]).standard_normal(out[name].shape)
        drawn = base * np.exp(spread * noise) if base else spread * noise
        out[name] = jnp.asarray(drawn.astype(out[name].dtype))
    for name, factor in factors.items():
        out[name] = (out[name] * factor).astype(out[name].dtype)
    return out
```

```python
import math
from contextlib import ExitStack

import numpy as np

import concourse.bass as bass
from concourse import mybir

F32 = mybir.dt.float32
F16 = mybir.dt.float16
BF16 = mybir.dt.bfloat16
U8 = mybir.dt.uint8
ALU = mybir.AluOpType
ACT = mybir.ActivationFunctionType
AX = mybir.AxisListType

P = 128
B, S, D = 8, 256, 512
TT = S // P
KD = D // P
E = 2048
KE = E // P
NTILES = B * TT
PAIRS = B // 2
HC, HW = 32, 8
CH = 1024

LN_SCALE = 2048.0
NORM = 32768.0
LN_EPS = 1e-5
NEG = -1e30



class Chain:

    def __init__(self, eng, sem):
        self.eng, self.sem, self.total, self.at = eng, sem, 0, None

    def step(self, ins):
        self.total += 1
        ins.then_inc(self.sem, 1)
        return ins

    def settle(self):
        value = self.total if self.at is None else self.at + (self.total - self.start)
        self.eng.wait_ge(self.sem, value)

    def link(self, ins):
        self.step(ins)
        self.settle()

    def enter(self, i, per, trips):
        self.start, self.per, self.trips = self.total, per, trips
        self.at = i * per + self.start

    def leave(self):
        assert self.total - self.start == self.per, (self.total - self.start, self.per)
        self.total = self.start + self.per * self.trips
        self.at = None


def build(nc, t):
    ctx = ExitStack()
    with ctx:
        def sb(name, shape, dt=F32):
            return ctx.enter_context(nc.sbuf_tensor(name, shape, dt))

        def sem(name):
            return ctx.enter_context(nc.semaphore(name))

        X = sb("x_stream", [P, NTILES, D])
        area_a = sb("area_a", [P, 12288])
        area_b = sb("area_b", [P, 12288])
        area_c = sb("area_c", [P, 8192])
        area_g = sb("area_g", [P, 5120])
        xn = sb("xn", [P, 2, TT, D])
        xTh = sb("xT_high", [P, 2, KD, S], F16)
        xTl = sb("xT_low", [P, 2, KD, S], F16)
        stage = sb("stage", [P, 2, CH])
        ident = sb("ident", [P, P])
        identb = sb("ident_bf", [P, P], BF16)
        ones = sb("ones", [P, P])
        stats = sb("stats", [P, TT, 6])
        mv = sb("mean_var", [P, TT, 2])
        rstd = sb("rstd", [P, TT])
        half_pow = sb("half_pow", [P, 16])
        eps_col = sb("eps_col", [P, TT])
        gates = sb("gates", [P, 8])
        sc = sb("scalars", [P, 96])
        part = sb("partial_sums", [P, 32])
        psum = ctx.enter_context(nc.psum_tensor("psum", [P, 8, 512], F32))

        def view(area, byte, shape, dt=F32):
            n = int(np.prod(shape)) * (4 if dt == F32 else 1 if dt == U8 else 2)
            v = area[:, byte // 4:(byte + n + 3) // 4]
            if dt != F32:
                v = v.bitcast(dt)
            if len(shape) == 2:
                v = v.rearrange("p (a b) -> p a b", a=shape[0])
            if len(shape) == 3:
                v = v.rearrange("p (a b c) -> p a b c", a=shape[0], b=shape[1])
            return v

        names = {}

        def S1(name):
            k = names.setdefault(name, len(names))
            return sc[:, k:k + 1]

        sems = {}

        def sig(name):
            if name not in sems:
                sems[name] = sem(name)
            return sems[name]

        def at(i, par, per, k):
            if i is None:
                return k
            return i * (2 * per) + (par * per + k)

        block = ctx.enter_context(nc.Block())

        vT = view(area_b, 0, [KD * B, S]).rearrange("p (k b) s -> p k b s", k=KD)
        cT = view(area_c, 0, [KD * B, S]).rearrange("p (k b) s -> p k b s", k=KD)
        kv = view(area_b, 32768, [2, KD, 512])
        ctx_nat = view(area_g, 0, [2, TT, D])
        toep = view(area_g, 8192, [2, 512])
        skip_prod = view(area_g, 12288, [TT, D])
        conv_tmp = view(area_g, 16384, [2, 512])
        skip_mat = view(area_a, 0, [TT, P])
        block_mask = view(area_a, 1024, [P])
        skip_col = view(area_a, 1536, [TT])

        def fcount(i, par, sub, n, k):
            if i is None:
                return (8 * sub + par) * n + k
            return i * (2 * n) + ((8 * sub + par) * n + k)

        def front_norm(dve, chain, i, par, sub, xi, buf):
            for t_ in range(TT):
                chain.step(nc.vector.bn_stats(stats[:, t_, :], X[:, xi * TT + t_, :]))
            chain.settle()
            dve.sem_inc(sig("stats_seen"), 1)
            for t_ in range(TT):
                nc.vector.bn_aggr(mv[:, t_, :], stats[:, t_, :]).then_inc(sig("front_stats"), 1)
            dve.wait_ge(sig("front_rstd"), fcount(i, par, sub, 1, 1))
            for t_ in range(TT):
                nc.vector.tensor_scalar(xn[:, buf, t_, :], X[:, xi * TT + t_, :], mv[:, t_, 0:1], rstd[:, t_:t_ + 1],
                                        ALU.subtract, ALU.mult).then_inc(sig("xn_ready"), 1)

        def front_rstd(pool, pchain, i, par, sub):
            pool.wait_ge(sig("front_stats"), fcount(i, par, sub, TT, TT))
            pchain.link(nc.gpsimd.tensor_tensor(rstd[:, :], mv[:, :, 1], eps_col[:, :], ALU.add))
            nc.gpsimd.tensor_tensor(rstd[:, :], rstd[:, :], half_pow[:, 0:TT], ALU.pow).then_inc(sig("front_rstd"), 1)

        def front_transpose(pe, i, par, sub, buf):
            for t_ in range(TT):
                pe.wait_ge(sig("xn_ready"), fcount(i, par, sub, TT, t_ + 1))
                pe.wait_ge(sig("front_bank_free"), fcount(i, par, sub, TT, t_ + 1))
                for k in range(KD):
                    last = nc.tensor.transpose(psum[:, 0, k * P:(k + 1) * P], xn[:, buf, t_, k * P:(k + 1) * P], ident[:, :])
                last.then_inc(sig("xT_ready"), 1)

        def front_high(act, i, par, sub, buf):
            for t_ in range(TT):
                act.wait_ge(sig("xT_ready"), fcount(i, par, sub, TT, t_ + 1))
                nc.scalar.activation(xTh[:, buf, :, t_ * P:(t_ + 1) * P], psum[:, 0, :].rearrange("p (k n) -> p k n", k=KD),
                                     ACT.Copy, scale=LN_SCALE).then_inc(sig("xT_high_ready"), 1)

        def front_low(dve, i, par, sub, buf):
            for t_ in range(TT):
                dve.wait_ge(sig("xT_high_ready"), fcount(i, par, sub - 1, TT, t_ + 1))
                nc.vector.scalar_tensor_tensor(out=xTl[:, buf, :, t_ * P:(t_ + 1) * P],
                                               in0=psum[:, 0, :].rearrange("p (k n) -> p k n", k=KD), scalar=LN_SCALE,
                                               in1=xTh[:, buf, :, t_ * P:(t_ + 1) * P], op0=ALU.mult,
                                               op1=ALU.subtract).then_inc(sig("front_bank_free"), 1)

        def front_done(pe, i, par, sub):
            pe.wait_ge(sig("front_bank_free"), fcount(i, par, sub, TT, TT + 1))

        def following(i, par):
            return i * 2 + 1 if par == 0 else ((i + 1) & 3) * 2

        plan = []
        PREP_NO = {1: 1, 3: 2, 5: 3, 6: 4}
        NORM_NO = {3: 1, 6: 2}

        def add_prep(sub, mats):
            steps = []
            m0 = len(names)
            for k, m in enumerate(mats):
                if m[2] != "sign":
                    for c in range(m[1]):
                        steps.append((len(plan) + len(steps), 1, k, c))
            n1 = len(steps)
            for k, m in enumerate(mats):
                for c in range(m[1]):
                    steps.append((len(plan) + len(steps), 2, k, c))
            plan.extend(steps)
            return mats, steps, n1

        def prep_load(sp, prep):
            mats, steps, n1 = prep
            for j, pas, k, c in steps:
                if j >= 2:
                    sp.wait_ge(sig("stage_free"), j - 1)
                sp.dma_start(stage[:, j % 2, :], t[mats[k][0]][:, c * CH:(c + 1) * CH]).then_inc(sig(f"stage_loaded{j % 2}"), 16)

        def prep_act(act, prep, sub, hi_count):
            mats, steps, n1 = prep
            col = 0
            scaled = False
            for j, pas, k, c in steps:
                kind = mats[k][2]
                if pas == 2 and kind == "ternary":
                    continue
                if pas == 2 and kind == "split" and not scaled:
                    act.wait_ge(sig("prep_scalars"), NORM_NO[sub])
                    scaled = True
                act.wait_ge(sig(f"stage_loaded{j % 2}"), 16 * (j // 2 + 1))
                if pas == 1:
                    nc.scalar.activation(stage[:, j % 2, :], stage[:, j % 2, :], ACT.Abs if kind == "ternary" else ACT.Square,
                                         accum_out=part[:, col:col + 1]).then_inc(sig("stage_free"), 1)
                    col += 1
                elif kind == "split":
                    nc.scalar.activation(mats[k][3][:, c * CH:(c + 1) * CH], stage[:, j % 2, :], ACT.Copy,
                                         scale=S1(f"s_{mats[k][0]}")).then_inc(sig("prep_high"), 1)
                else:
                    nc.scalar.activation(mats[k][3][:, c * CH:(c + 1) * CH], stage[:, j % 2, :], ACT.Sign).then_inc(sig("stage_free"), 1)

        def prep_dve(dve, chain, prep, sub, hi_count):
            mats, steps, n1 = prep
            if n1:
                dve.wait_ge(sig("stage_free"), steps[0][0] + n1)
                col = 0
                nm = 0
                for m in mats:
                    if m[2] != "sign":
                        chain.step(nc.vector.reduce_sum(sc[:, 80 + nm:81 + nm], part[:, col:col + m[1]], AX.X))
                        col += m[1]
                        nm += 1
                chain.settle()
                nc.vector.tensor_copy(part[:, 24:24 + nm], sc[:, 80:80 + nm]).then_inc(sig("prep_sums"), 1)
                dve.wait_ge(sig("prep_total"), PREP_NO[sub])
                chain.link(nc.vector.tensor_scalar(sc[:, 80:80 + nm], psum[:, 7, 0:nm], 1e-30, None, ALU.max))
                if mats[0][2] == "ternary":
                    for k, m in enumerate(mats):
                        n = P * CH * m[1]
                        chain.step(nc.vector.tensor_scalar(S1(f"mean_{m[0]}"), psum[:, 7, k:k + 1], 1.0 / n, None, ALU.mult))
                        chain.step(nc.vector.tensor_scalar(S1(f"up_{m[0]}"), psum[:, 7, k:k + 1], 0.5 / n, 0.5e-8, ALU.mult, ALU.add))
                        chain.step(nc.vector.tensor_scalar(S1(f"dn_{m[0]}"), psum[:, 7, k:k + 1], -0.5 / n, -0.5e-8, ALU.mult, ALU.add))
                    chain.settle()
                else:
                    nc.vector.tensor_copy(sc[:, 88:88 + nm], sc[:, 80:80 + nm]).then_inc(sig("prep_squares"), 1)
                    dve.wait_ge(sig("prep_roots"), NORM_NO[sub])
                    for k, m in enumerate(mats):
                        chain.step(nc.vector.tensor_scalar(S1(f"s_{m[0]}"), sc[:, 88 + k:89 + k], NORM, None, ALU.mult))
                        chain.step(nc.vector.scalar_tensor_tensor(out=S1(f"inv_{m[0]}"), in0=sc[:, 88 + k:89 + k], scalar=1.0 / NORM,
                                                                  in1=sc[:, 80 + k:81 + k], op0=ALU.mult, op1=ALU.mult))
                    chain.settle()
                    nc.vector.tensor_copy(part[:, 24:25], part[:, 24:25]).then_inc(sig("prep_scalars"), 1)
            for j, pas, k, c in steps:
                if pas == 1 or mats[k][2] == "sign":
                    continue
                m = mats[k]
                if m[2] == "ternary":
                    dve.wait_ge(sig(f"stage_loaded{j % 2}"), 16 * (j // 2 + 1))
                    chain.link(nc.vector.tensor_scalar(prep_tmp[:, j % 2, :], stage[:, j % 2, :], S1(f"dn_{m[0]}"), None, ALU.is_lt))
                    nc.vector.scalar_tensor_tensor(out=m[3][:, c * CH:(c + 1) * CH], in0=stage[:, j % 2, :],
                                                   scalar=S1(f"up_{m[0]}"), in1=prep_tmp[:, j % 2, :], op0=ALU.is_gt,
                                                   op1=ALU.subtract).then_inc(sig("stage_free"), 1)
                else:
                    hi_count[0] += 1
                    dve.wait_ge(sig("prep_high"), hi_count[0])
                    nc.vector.scalar_tensor_tensor(out=m[4][:, c * CH:(c + 1) * CH], in0=stage[:, j % 2, :],
                                                   scalar=S1(f"s_{m[0]}"), in1=m[3][:, c * CH:(c + 1) * CH], op0=ALU.mult,
                                                   op1=ALU.subtract).then_inc(sig("stage_free"), 1)

        def prep_pe(pe, sub, nm):
            pe.wait_ge(sig("prep_sums"), PREP_NO[sub])
            nc.tensor.matmul(psum[:, 7, 0:nm], ones[:, :], part[:, 24:24 + nm], start=True, stop=True).then_inc(sig("prep_total"), 1)

        def prep_pool(pool, sub, nm):
            pool.wait_ge(sig("prep_squares"), NORM_NO[sub])
            nc.gpsimd.tensor_tensor(sc[:, 88:88 + nm], sc[:, 88:88 + nm], half_pow[:, 0:nm], ALU.pow).then_inc(sig("prep_roots"), 1)

        prep_tmp = view(area_g, 16384, [2, CH], F16)

        def flat(area, byte, n):
            return view(area, byte, [n], F16)

        prep1 = add_prep(1, [("w0_up", 8, "ternary", flat(area_a, 0, 8192), None),
                             ("w0_gate", 8, "ternary", flat(area_a, 16384, 8192), None),
                             ("w0_down", 8, "ternary", flat(area_a, 32768, 8192), None)])
        w0_up = view(area_a, 0, [KD, E], F16)
        w0_gate = view(area_a, 16384, [KD, E], F16)
        w0_down = view(area_a, 32768, [KE, D], F16)
        hTh = view(area_b, 0, [KE, S], F16)
        hTl = view(area_b, 8192, [KE, S], F16)
        th = view(area_b, 16384, [2, 512])
        act_a = view(area_b, 20480, [2, 512])
        hid = view(area_b, 24576, [2, 512])

        def sp_constants(sp):
            for name, n in (("front_bank_free", 1), ("skip_ps_ready", TT), ("skip_added", 2 * TT), ("kv_used", 2),
                            ("y_drained", 2 * KD)):
                sp.sem_inc(sig(name), n)
            for dst, src in ((ident[:, :], "c_ident"), (block_mask, "c_block"), (skip_col, "skip"), (gates[:, :], "gates")):
                a = t[src]
                sp.dma_start(dst, a.partition_broadcast(P) if src == "gates" else a).then_inc(sig("constants_loaded"), 16)

        def sp_stage0(sp):
            xd = t["x"].rearrange("(n p) d -> p n d", p=P)
            for c in range(4):
                sp.dma_start(X[:, c * 4:(c + 1) * 4, :], xd[:, c * 4:(c + 1) * 4, :]).then_inc(sig("x_loaded"), 16)
            for k in range(KD):
                sp.dma_start(cT[:, k, :, :], t["ctxT"][:, k]).then_inc(sig("ctxT_loaded"), 16)
            cn = t["ctx"].rearrange("(b t p) d -> p b t d", p=P, t=TT)
            with sp.Fori(0, PAIRS) as i:
                for par in range(2):
                    sp.wait_ge(sig("skip_added"), at(i, par, TT, TT))
                    sp.dma_start(ctx_nat[:, par], cn[:, i * 2 + par]).then_inc(sig(f"ctx_nat_loaded{par}"), 16)
            with sp.Fori(0, HC // 2) as i:
                for par in range(2):
                    sp.wait_ge(sig("kv_used"), i * 2 + (par + 1))
                    sp.dma_start(toep[:, par, :], t["toeplitz"][i * 2 + par]).then_inc(sig(f"toep_loaded{par}"), 16)

        def pool_stage0(pool, pc):
            with pool.Fori(0, PAIRS) as i:
                for par in range(2):
                    pc.enter(i, 2, PAIRS) if par == 0 else None
                    front_rstd(pool, pc, i, par, 0)
                    pool.wait_ge(sig(f"ctx_nat_loaded{par}"), i * 16 + 16)
                    for t_ in range(TT):
                        pool.wait_ge(sig("xn_ready"), at(i, par, TT, t_ + 1))
                        pool.wait_ge(sig("skip_ps_ready"), at(i, par, TT, t_ + 1))
                        nc.gpsimd.tensor_tensor(skip_prod[:, t_, :], xn[:, par, t_, :], ctx_nat[:, par, t_, :],
                                                ALU.mult).then_inc(sig("skip_prod_ready"), 1)
                pc.leave()
            pool.wait_ge(sig("front_bank_free"), 2 * B + 1)
            pool.wait_ge(sig("ctxT_loaded"), 16 * KD)
            with pool.Fori(0, HC // 2) as i:
                for par in range(2):
                    pool.wait_ge(sig("kv_used"), i * 2 + (par + 1))
                    for k in range(KD):
                        cols = bass.ds((i * 2 + par) * HW, HW)
                        nc.gpsimd.tensor_tensor(
                            kv[:, par, k, :].rearrange("p (b i j) -> p b i j", b=B, i=HW),
                            vT[:, k, :, cols].unsqueeze(3).broadcast_to([P, B, HW, HW]),
                            cT[:, k, :, cols].unsqueeze(2).broadcast_to([P, B, HW, HW]), ALU.mult).then_inc(sig("kv_ready"), 1)

        def dve_stage0(dve, dc):
            dve.wait_ge(sig("constants_loaded"), 64)
            for t_ in range(TT):
                dc.step(nc.vector.tensor_scalar(skip_mat[:, t_, :], block_mask, skip_col[:, t_:t_ + 1], None, ALU.mult))
            dc.step(nc.vector.tensor_copy(identb[:, :], ident[:, :]))
            dc.settle()
            nc.vector.memset(ones[:, :], 1.0).then_inc(sig("tables_ready"), 1)
            dve.wait_ge(sig("gates_ready"), 1)
            dve.wait_ge(sig("x_loaded"), 64)
            with dve.Fori(0, PAIRS) as i:
                dc.enter(i, 8, PAIRS)
                for par in range(2):
                    front_norm(dve, dc, i, par, 0, i * 2 + par, par)
                    for t_ in range(TT):
                        dve.wait_ge(sig("xT_ready"), at(i, par, TT, t_ + 1))
                        nc.vector.tensor_copy(vT[:, :, i * 2 + par, t_ * P:(t_ + 1) * P],
                                              psum[:, 0, :].rearrange("p (k n) -> p k n", k=KD)).then_inc(sig("front_bank_free"), 1)
                    for t_ in range(TT):
                        dve.wait_ge(sig("skip_ps_ready"), at(i, par, TT, t_ + 1 + TT))
                        dc.link(nc.vector.tensor_tensor(conv_tmp[:, t_, :], psum[:, 2 + t_, :], ctx_nat[:, par, t_, :], ALU.mult))
                        xt = X[:, (i * 2 + par) * TT + t_, :]
                        nc.vector.scalar_tensor_tensor(out=xt, in0=conv_tmp[:, t_, :], scalar=gates[:, 0:1], in1=xt,
                                                       op0=ALU.mult, op1=ALU.add).then_inc(sig("skip_added"), 1)
                dc.leave()
            dve.wait_ge(sig("skip_added"), 2 * TT + TT * B)
            with dve.Fori(0, HC // 2) as i:
                dc.enter(i, 6, HC // 2)
                for par in range(2):
                    for m in range(KD):
                        cols = bass.ds((i * 2 + par) * HW, HW)
                        tmp = conv_tmp[:, m % 2, :]
                        dve.wait_ge(sig("y_ready"), at(i, par, KD, m + 1))
                        nc.vector.tensor_tensor(
                            tmp.rearrange("p (b i j) -> p b i j", b=B, i=HW),
                            psum[:, 4 * par + m, :].rearrange("p (b i j) -> p b i j", b=B, i=HW),
                            cT[:, m, :, cols].unsqueeze(3).broadcast_to([P, B, HW, HW]), ALU.mult).then_inc(sig("y_drained"), 1)
                        dve.wait_ge(sig("y_drained"), at(i, par, KD, m + 1 + 2 * KD))
                        r = nc.vector.reduce_sum(vT[:, m, :, cols], tmp.rearrange("p (b i j) -> p b j i", b=B, i=HW), AX.X)
                        if m == KD - 1:
                            r.then_inc(sig("conv_reduced"), 1)
                        else:
                            dc.step(r)
                dc.leave()
            for n in range(NTILES):
                dve.wait_ge(sig("conv_T"), n + 1)
                nc.vector.scalar_tensor_tensor(out=X[:, n, :], in0=psum[:, 2 + n % 4, :], scalar=gates[:, 0:1], in1=X[:, n, :],
                                               op0=ALU.mult, op1=ALU.add).then_inc(sig("conv_added"), 1)
            dve.wait_ge(sig("conv_added"), NTILES)

        def pe_stage0(pe):
            pe.wait_ge(sig("tables_ready"), 1)
            with pe.Fori(0, PAIRS) as i:
                for par in range(2):
                    front_transpose(pe, i, par, 0, par)
                    for t_ in range(TT):
                        pe.wait_ge(sig("skip_prod_ready"), at(i, par, TT, t_ + 1))
                        pe.wait_ge(sig("skip_added"), at(i, par, TT, t_ + 1 + TT))
                        nc.tensor.matmul(psum[:, 2 + t_, :], skip_mat[:, t_, :], skip_prod[:, t_, :], start=True,
                                         stop=True).then_inc(sig("skip_ps_ready"), 1)
            pe.wait_ge(sig("skip_added"), 2 * TT + TT * B)
            with pe.Fori(0, HC // 2) as i:
                for par in range(2):
                    pe.wait_ge(sig(f"toep_loaded{par}"), i * 16 + 16)
                    for m in range(KD):
                        pe.wait_ge(sig("kv_ready"), at(i, par, KD, m + 1))
                        pe.wait_ge(sig("y_drained"), at(i, par, KD, m + 1))
                        for k in range(m + 1):
                            last = nc.tensor.matmul(psum[:, 4 * par + m, :], toep[:, par, (m - k) * P:(m - k + 1) * P],
                                                    kv[:, par, k, :], start=(k == 0), stop=(k == m))
                        last.then_inc(sig("y_ready"), 1)
                    pe.wait_ge(sig("y_ready"), at(i, par, KD, KD))
                    pe.sem_inc(sig("kv_used"), 1)
            pe.wait_ge(sig("conv_reduced"), HC)
            for n in range(NTILES):
                if n >= 4:
                    pe.wait_ge(sig("conv_added"), n - 3)
                for k in range(KD):
                    last = nc.tensor.transpose(psum[:, 2 + n % 4, k * P:(k + 1) * P],
                                               vT[:, k, n // TT, (n % TT) * P:(n % TT + 1) * P], ident[:, :])
                last.then_inc(sig("conv_T"), 1)

        def act_stage0(act):
            act.wait_ge(sig("constants_loaded"), 64)
            nc.scalar.activation(gates[:, :], gates[:, :], ACT.Tanh).then_inc(sig("gates_ready"), 1)
            act.wait_ge(sig("ctxT_loaded"), 16 * KD)
            for k in range(KD):
                nc.scalar.activation(view(area_a, 8192 + 8192 * k, [2048]), cT[:, k].rearrange("p b s -> p (b s)"), ACT.Square,
                                     accum_out=part[:, 16 + k:17 + k]).then_inc(sig("ctx_squares_ready"), 1)

        NJ = KE // 2

        def sp_stage1(sp):
            prep_load(sp, prep1)
            sp.sem_inc(sig("hid_ready"), 2)
            sp.sem_inc(sig("ffn0_added"), TT)

        def pool_stage1(pool, pc):
            front_rstd(pool, pc, None, 0, 1)
            with pool.Fori(0, PAIRS) as i:
                pc.enter(i, 2, PAIRS)
                for par in range(2):
                    front_rstd(pool, pc, i, par + 1, 1)
                pc.leave()

        def pe_stage1(pe):
            prep_pe(pe, 1, 3)
            pe.wait_ge(sig("weights_ready"), 1)
            front_transpose(pe, None, 0, 1, 0)

            def down(i, par, j):
                for t_ in range(TT):
                    if j == 0:
                        pe.wait_ge(sig("ffn0_added"), at(i, par, TT, t_ + 1))
                    if t_ == 0:
                        pe.wait_ge(sig("hid_low_ready"), at(i, par, NJ, j + 1))
                    for k in (2 * j, 2 * j + 1):
                        for n, h in enumerate((hTh, hTl)):
                            last = nc.tensor.matmul(psum[:, 6 + t_, :], h[:, k, t_ * P:(t_ + 1) * P], w0_down[:, k, :],
                                                    start=(k == 0 and n == 0), stop=(k == KE - 1 and n == 1))
                    if j == NJ - 1:
                        last.then_inc(sig("down_ready"), 1)

            with pe.Fori(0, PAIRS) as i:
                for par in range(2):
                    front_done(pe, i, par, 1)
                    for j in range(NJ):
                        pe.wait_ge(sig("hid_ready"), at(i, par, NJ, j + 1))
                        for side, w in ((0, w0_up), (1, w0_gate)):
                            bank = 2 + 2 * (j % 2) + side
                            for m in (2 * j, 2 * j + 1):
                                out = psum[:, bank, (m % 2) * S:(m % 2 + 1) * S]
                                for k in range(KD):
                                    for n, xt in enumerate((xTh, xTl)):
                                        last = nc.tensor.matmul(out, w[:, k, m * P:(m + 1) * P], xt[:, par, k, :],
                                                                start=(k == 0 and n == 0), stop=(k == KD - 1 and n == 1))
                            last.then_inc(sig("up_gate_ready"), 1)
                        if j >= 2:
                            down(i, par, j - 2)
                        if j == 4:
                            front_transpose(pe, i, par + 1, 1, 1 - par)
                    down(i, par, NJ - 2)
                    down(i, par, NJ - 1)

        def act_stage1(act):
            prep_act(act, prep1, 1, None)
            front_high(act, None, 0, 1, 0)
            act.wait_ge(sig("weights_ready"), 1)
            with act.Fori(0, PAIRS) as i:
                for par in range(2):
                    for j in range(NJ):
                        act.wait_ge(sig("up_gate_ready"), at(i, par, 2 * NJ, 2 * j + 1))
                        nc.scalar.activation(th[:, j % 2, :], psum[:, 2 + 2 * (j % 2), :], ACT.Tanh,
                                             scale=S1("half_up")).then_inc(sig("tanh_ready"), 1)
                        if j == 4:
                            front_high(act, i, par + 1, 1, 1 - par)
                        act.wait_ge(sig("hid_ready"), at(i, par, NJ, j + 3))
                        nc.scalar.activation(hTh[:, 2 * j:2 * j + 2, :], hid[:, j % 2, :].rearrange("p (m s) -> p m s", m=2),
                                             ACT.Copy, scale=2.0 ** -26).then_inc(sig("hid_high_ready"), 1)

        def dve_stage1(dve, dc):
            prep_dve(dve, dc, prep1, 1, None)
            dc.step(nc.vector.tensor_scalar(S1("half_up"), S1("mean_w0_up"), 1e-8, 0.5 / LN_SCALE, ALU.add, ALU.mult))
            dc.link(nc.vector.tensor_scalar(S1("ffn0"), S1("mean_w0_up"), 1e-8, 8.0, ALU.add, ALU.mult))
            dc.step(nc.vector.tensor_scalar(part[:, 30:31], S1("mean_w0_gate"), 1e-8, S1("ffn0"), ALU.add, ALU.mult))
            dc.settle()
            dc.link(nc.vector.tensor_scalar(part[:, 31:32], S1("mean_w0_down"), 1e-8, part[:, 30:31], ALU.add, ALU.mult))
            dc.link(nc.vector.tensor_tensor(S1("ffn0"), part[:, 31:32], gates[:, 4:5], ALU.mult))
            dve.wait_ge(sig("stage_free"), len(prep1[1]))
            nc.vector.tensor_copy(part[:, 30:31], S1("ffn0")).then_inc(sig("weights_ready"), 1)
            front_norm(dve, dc, None, 0, 1, 0, 0)
            front_low(dve, None, 0, 1, 0)
            with dve.Fori(0, PAIRS) as i:
                dc.enter(i, 20, PAIRS)
                for par in range(2):
                    front_norm(dve, dc, i, par + 1, 1, following(i, par), 1 - par)
                    for j in range(NJ):
                        dve.wait_ge(sig("tanh_ready"), at(i, par, NJ, j + 1))
                        dve.wait_ge(sig("up_gate_ready"), at(i, par, 2 * NJ, 2 * j + 2))
                        dc.link(nc.vector.scalar_tensor_tensor(out=act_a[:, j % 2, :], in0=th[:, j % 2, :], scalar=1.0,
                                                               in1=psum[:, 2 + 2 * (j % 2), :], op0=ALU.add, op1=ALU.mult))
                        nc.vector.tensor_tensor(hid[:, j % 2, :], act_a[:, j % 2, :], psum[:, 3 + 2 * (j % 2), :],
                                                ALU.mult).then_inc(sig("hid_ready"), 1)
                        if j == 4:
                            front_low(dve, i, par + 1, 1, 1 - par)
                        dve.wait_ge(sig("hid_high_ready"), at(i, par, NJ, j + 1))
                        nc.vector.scalar_tensor_tensor(out=hTl[:, 2 * j:2 * j + 2, :],
                                                       in0=hid[:, j % 2, :].rearrange("p (m s) -> p m s", m=2),
                                                       scalar=2.0 ** -26, in1=hTh[:, 2 * j:2 * j + 2, :], op0=ALU.mult,
                                                       op1=ALU.subtract).then_inc(sig("hid_low_ready"), 1)
                    for t_ in range(TT):
                        xt = X[:, (i * 2 + par) * TT + t_, :]
                        dve.wait_ge(sig("down_ready"), at(i, par, TT, t_ + 1))
                        nc.vector.scalar_tensor_tensor(out=xt, in0=psum[:, 6 + t_, :], scalar=S1("ffn0"), in1=xt,
                                                       op0=ALU.mult, op1=ALU.add).then_inc(sig("ffn0_added"), 1)
                dc.leave()

        wkv_w = S1("w_0"); [S1(f"w_{k}") for k in range(1, KD)]
        wkv_u = S1("u_0"); [S1(f"u_{k}") for k in range(1, KD)]
        W0, U0 = names["w_0"], names["u_0"]
        flat4 = "p (k s) -> p k s"
        wk_k = view(area_b, 0, [KD, S])
        wk_o = view(area_b, 4096, [KD, S + 1])
        wk_uk = view(area_b, 8208, [KD, S])
        wk_no = view(area_b, 12304, [KD, S])
        wk_d = view(area_b, 16400, [4, KD, S])
        wk_t1 = view(area_b, 32784, [KD, S])
        wk_t2 = view(area_b, 36880, [KD, S])
        wk_p = view(area_b, 40976, [KD, S + 1])
        wk_t3 = view(area_g, 0, [KD, S])
        wk_q = view(area_g, 4096, [KD, S + 1])
        wk_l = view(area_g, 8208, [KD, S])
        wk_v = view(area_g, 12304, [KD, S])
        wk_y = wk_uk

        def sp_stage2(sp):
            sp.sem_inc(sig("wkv_added"), TT)
            sp.wait_ge(sig("weights_ready"), 1)
            for dst, name in ((sc[:, W0:W0 + KD], "wkv_w"), (sc[:, U0:U0 + KD], "wkv_u")):
                sp.dma_start(dst, t[name]).then_inc(sig("wkv_constants"), 16)
            with sp.Fori(0, PAIRS) as i:
                for par in range(2):
                    sp.wait_ge(sig("wkv_added"), at(i, par, TT, TT))
                    sp.dma_start(wk_v, t["ctxT"][:, :, i * 2 + par, :]).then_inc(sig("wkv_v_loaded"), 16)

        def pool_stage2(pool, pc):
            with pool.Fori(0, PAIRS) as i:
                pc.enter(i, 2, PAIRS)
                for par in range(2):
                    pool.wait_ge(sig("wkv_no_ready"), at(i, par, 1, 1))
                    nc.gpsimd.tensor_tensor(wk_d[:, 0], wk_o[:, :, 0:S], wk_no, ALU.subtract).then_inc(sig("wkv_d_ready"), 1)
                    nc.gpsimd.tensor_tensor(wk_d[:, 1], wk_uk, wk_no, ALU.subtract).then_inc(sig("wkv_d_ready"), 1)
                    nc.gpsimd.tensor_tensor(wk_d[:, 3], wk_k, wk_o[:, :, 1:S + 1], ALU.subtract).then_inc(sig("wkv_d_ready"), 1)
                    front_rstd(pool, pc, i, par + 1, 2)
                    pool.wait_ge(sig("wkv_v_loaded"), i * 32 + (par * 16 + 16))
                    pool.wait_ge(sig("wkv_exp_ready"), at(i, par, 2, 1))
                    nc.gpsimd.tensor_tensor(wk_t1, wk_d[:, 3], wk_v, ALU.mult).then_inc(sig("wkv_ev2_ready"), 1)
                    pool.wait_ge(sig("wkv_exp_ready"), at(i, par, 2, 2))
                    nc.gpsimd.tensor_tensor(wk_t2, wk_d[:, 1], wk_v, ALU.mult).then_inc(sig("wkv_ev_ready"), 1)
                pc.leave()

        def act_stage2(act):
            act.wait_ge(sig("wkv_constants"), 32)
            with act.Fori(0, PAIRS) as i:
                for par in range(2):
                    act.wait_ge(sig("wkv_added"), at(i, par, TT, TT))
                    act.wait_ge(sig("front_bank_free"), fcount(i, par, 2, TT, TT + 1))
                    nc.scalar.activation(wk_l, xTl[:, par], ACT.Copy, scale=1.0 / LN_SCALE).then_inc(sig("wkv_l_ready"), 1)
                    act.wait_ge(sig("wkv_k_ready"), at(i, par, 1, 1))
                    for k in range(KD):
                        nc.scalar.activation(wk_uk[:, k, :], wk_k[:, k, :], ACT.Identity,
                                             bias=sc[:, U0 + k:U0 + k + 1]).then_inc(sig("wkv_uk_ready"), 1)
                    act.wait_ge(sig("wkv_d_ready"), at(i, par, 3, 3))
                    act.wait_ge(sig("wkv_d2_ready"), at(i, par, KD, KD))
                    d = wk_d[:, 2:4]
                    nc.scalar.activation(d, d, ACT.Exp).then_inc(sig("wkv_exp_ready"), 1)
                    d = wk_d[:, 0:2]
                    nc.scalar.activation(d, d, ACT.Exp).then_inc(sig("wkv_exp_ready"), 1)
                    front_high(act, i, par + 1, 2, 1 - par)

        def dve_stage2(dve, dc):
            dve.wait_ge(sig("wkv_constants"), 32)
            dve.wait_ge(sig("ffn0_added"), TT * B + TT)
            for z, v in ((wk_o, -1e38), (wk_p, 0.0), (wk_q, 0.0)):
                dc.step(nc.vector.memset(z[:, :, 0:1], v))
            dc.settle()
            with dve.Fori(0, PAIRS) as i:
                dc.enter(i, 38, PAIRS)
                for par in range(2):
                    dve.wait_ge(sig("wkv_l_ready"), at(i, par, 1, 1))
                    nc.vector.scalar_tensor_tensor(out=wk_k, in0=xTh[:, par], scalar=1.0 / LN_SCALE, in1=wk_l, op0=ALU.mult,
                                                   op1=ALU.add).then_inc(sig("wkv_k_ready"), 1)
                    dve.wait_ge(sig("wkv_k_ready"), at(i, par, 1, 1))
                    for k in range(KD):
                        dc.step(nc.vector.tensor_tensor_scan(wk_o[:, k, 1:S + 1], sc[:, W0 + k:W0 + k + 1].broadcast_to([P, S]),
                                                             wk_k[:, k, :], -1e38, ALU.add, ALU.max))
                    dve.wait_ge(sig("wkv_uk_ready"), at(i, par, KD, KD))
                    dc.settle()
                    nc.vector.tensor_tensor(wk_no, wk_o[:, :, 0:S], wk_uk, ALU.max).then_inc(sig("wkv_no_ready"), 1)
                    for k in range(KD):
                        nc.vector.scalar_tensor_tensor(out=wk_d[:, 2, k, :], in0=wk_o[:, k, 0:S], scalar=sc[:, W0 + k:W0 + k + 1],
                                                       in1=wk_o[:, k, 1:S + 1], op0=ALU.add,
                                                       op1=ALU.subtract).then_inc(sig("wkv_d2_ready"), 1)
                    front_norm(dve, dc, i, par + 1, 2, following(i, par), 1 - par)
                    dve.wait_ge(sig("wkv_exp_ready"), at(i, par, 2, 1))
                    for k in range(KD):
                        dc.step(nc.vector.tensor_tensor_scan(wk_q[:, k, 1:S + 1], wk_d[:, 2, k, :], wk_d[:, 3, k, :], 0.0,
                                                             ALU.mult, ALU.add))
                    dve.wait_ge(sig("wkv_ev2_ready"), at(i, par, 1, 1))
                    for k in range(KD):
                        dc.step(nc.vector.tensor_tensor_scan(wk_p[:, k, 1:S + 1], wk_d[:, 2, k, :], wk_t1[:, k, :], 0.0,
                                                             ALU.mult, ALU.add))
                    front_low(dve, i, par + 1, 2, 1 - par)
                    dve.wait_ge(sig("wkv_exp_ready"), at(i, par, 2, 2))
                    dc.settle()
                    dc.step(nc.vector.tensor_tensor(wk_t3, wk_d[:, 0], wk_q[:, :, 0:S], ALU.mult))
                    dc.link(nc.vector.tensor_tensor(wk_no, wk_d[:, 0], wk_p[:, :, 0:S], ALU.mult))
                    dc.link(nc.vector.tensor_tensor(wk_t3, wk_t3, wk_d[:, 1], ALU.add))
                    dc.step(nc.vector.reciprocal(wk_t3, wk_t3))
                    dve.wait_ge(sig("wkv_ev_ready"), at(i, par, 1, 1))
                    dc.link(nc.vector.tensor_tensor(wk_no, wk_no, wk_t2, ALU.add))
                    nc.vector.tensor_tensor(wk_y, wk_no, wk_t3, ALU.mult).then_inc(sig("wkv_y_ready"), 1)
                    for t_ in range(TT):
                        xt = X[:, (i * 2 + par) * TT + t_, :]
                        dve.wait_ge(sig("wkv_yT_ready"), at(i, par, TT, t_ + 1))
                        nc.vector.scalar_tensor_tensor(out=xt, in0=psum[:, 2 + t_, :], scalar=gates[:, 1:2], in1=xt,
                                                       op0=ALU.mult, op1=ALU.add).then_inc(sig("wkv_added"), 1)
                dc.leave()

        def pe_stage2(pe):
            with pe.Fori(0, PAIRS) as i:
                for par in range(2):
                    front_transpose(pe, i, par + 1, 2, 1 - par)
                    pe.wait_ge(sig("wkv_y_ready"), at(i, par, 1, 1))
                    pe.wait_ge(sig("wkv_added"), at(i, par, TT, TT))
                    for t_ in range(TT):
                        for k in range(KD):
                            last = nc.tensor.transpose(psum[:, 2 + t_, k * P:(k + 1) * P], wk_y[:, k, t_ * P:(t_ + 1) * P], ident[:, :])
                        last.then_inc(sig("wkv_yT_ready"), 1)

        raw34 = view(area_a, 0, [5120])
        w34h, w34l = flat(area_c, 0, 5120), flat(area_c, 10240, 5120)
        w2_o = view(area_c, 20480, [KD, D])
        PARTS34 = (("w1", 2048), ("w2_q", 2048), ("w2_kv", 1024))
        offs34 = {"w1": 0, "w2_q": 2048, "w2_kv": 4096}

        def w34(name, n):
            o = offs34[name]
            return [w[:, o:o + KD * n].rearrange("p (k n) -> p k n", k=KD) for w in (w34h, w34l)]

        w1_scale = view(area_g, 0, [D])
        ffn1_bias = view(area_g, 2048, [D])
        square_junk = view(area_g, 4096, [2048])

        def row(name):
            return t[name].partition_broadcast(P)

        def sp_stage3(sp):
            sp.wait_ge(sig("wkv_added"), TT * B + TT)
            sp.dma_start(w1_scale, row("w1_scale")).then_inc(sig("raw34_loaded"), 16)
            sp.dma_start(ffn1_bias, row("w1_bias")).then_inc(sig("raw34_loaded"), 16)
            for name, n in PARTS34:
                sp.dma_start(raw34[:, offs34[name]:offs34[name] + n], t[name]).then_inc(sig("raw34_loaded"), 16)
            sp.dma_start(view(area_c, 20480, [2048]), t["w2_o"]).then_inc(sig("raw34_loaded"), 16)
            sp.sem_inc(sig("ffn1_added"), TT)

        def pool_stage3(pool, pc):
            prep_pool(pool, 3, 4)
            with pool.Fori(0, PAIRS) as i:
                pc.enter(i, 2, PAIRS)
                for par in range(2):
                    front_rstd(pool, pc, i, par + 1, 3)
                pc.leave()

        def act_stage3(act):
            act.wait_ge(sig("raw34_scaled"), 1)
            for m, (name, n) in enumerate(PARTS34):
                o = offs34[name]
                nc.scalar.activation(square_junk[:, 0:n], raw34[:, o:o + n], ACT.Square,
                                     accum_out=part[:, m:m + 1]).then_inc(sig("square34_ready"), 1)
                act.wait_ge(sig("square34_ready"), m + 1)
            act.wait_ge(sig("prep_scalars"), NORM_NO[3])
            for name, n in PARTS34:
                o = offs34[name]
                nc.scalar.activation(w34h[:, o:o + n], raw34[:, o:o + n], ACT.Copy, scale=S1(f"s_{name}")).then_inc(sig("high34_ready"), 1)
            with act.Fori(0, PAIRS) as i:
                for par in range(2):
                    front_high(act, i, par + 1, 3, 1 - par)

        def norms(dve, dc, sub, mats, source, col):
            nm = len(mats)
            nc.vector.tensor_copy(part[:, 24:24 + nm], source).then_inc(sig("prep_sums"), 1)
            dve.wait_ge(sig("prep_total"), PREP_NO[sub])
            dc.link(nc.vector.tensor_scalar(sc[:, 80:80 + nm], psum[:, 7, 0:nm], 1e-30, None, ALU.max))
            nc.vector.tensor_copy(sc[:, 88:88 + nm], sc[:, 80:80 + nm]).then_inc(sig("prep_squares"), 1)
            dve.wait_ge(sig("prep_roots"), NORM_NO[sub])
            for k, m in enumerate(mats):
                dc.step(nc.vector.tensor_scalar(S1(f"s_{m}"), sc[:, 88 + k:89 + k], NORM, None, ALU.mult))
                dc.step(nc.vector.scalar_tensor_tensor(out=S1(f"inv_{m}"), in0=sc[:, 88 + k:89 + k], scalar=1.0 / NORM,
                                                       in1=sc[:, 80 + k:81 + k], op0=ALU.mult, op1=ALU.mult))
            dc.settle()

        def dve_stage3(dve, dc):
            dve.wait_ge(sig("raw34_loaded"), 16 * 6)
            w = raw34[:, 0:KD * D].rearrange("p (k n) -> p k n", k=KD)
            dc.step(nc.vector.tensor_tensor(w, w, w1_scale.unsqueeze(1).broadcast_to([P, KD, D]), ALU.mult))
            dc.settle()
            nc.vector.tensor_scalar(ffn1_bias, ffn1_bias, gates[:, 5:6], None, ALU.mult).then_inc(sig("raw34_scaled"), 1)
            dve.wait_ge(sig("square34_ready"), 3)
            dve.wait_ge(sig("ctx_squares_ready"), KD)
            dc.link(nc.vector.reduce_sum(part[:, 3:4], part[:, 16:16 + KD], AX.X))
            norms(dve, dc, 3, [m for m, _ in PARTS34] + ["ctx"], part[:, 0:4], 0)
            nc.vector.scalar_tensor_tensor(out=S1("ffn1"), in0=S1("inv_w1"), scalar=1.0 / LN_SCALE, in1=gates[:, 5:6],
                                           op0=ALU.mult, op1=ALU.mult).then_inc(sig("prep_scalars"), 1)
            for m, (name, n) in enumerate(PARTS34):
                o = offs34[name]
                dve.wait_ge(sig("high34_ready"), m + 1)
                nc.vector.scalar_tensor_tensor(out=w34l[:, o:o + n], in0=raw34[:, o:o + n], scalar=S1(f"s_{name}"),
                                               in1=w34h[:, o:o + n], op0=ALU.mult, op1=ALU.subtract).then_inc(sig("low34_ready"), 1)
            dve.wait_ge(sig("low34_ready"), 3)
            with dve.Fori(0, PAIRS) as i:
                dc.enter(i, 8, PAIRS)
                for par in range(2):
                    front_norm(dve, dc, i, par + 1, 3, following(i, par), 1 - par)
                    front_low(dve, i, par + 1, 3, 1 - par)
                    for t_ in range(TT):
                        xt = X[:, (i * 2 + par) * TT + t_, :]
                        dve.wait_ge(sig("ffn1_ready"), at(i, par, TT, t_ + 1))
                        nc.vector.scalar_tensor_tensor(out=xt, in0=psum[:, 2 + t_, :], scalar=S1("ffn1"), in1=xt,
                                                       op0=ALU.mult, op1=ALU.add).then_inc(sig("ffn1_added"), 1)
                    for t_ in range(TT):
                        xt = X[:, (i * 2 + par) * TT + t_, :]
                        dve.wait_ge(sig("ffn1_added"), at(i, par, TT, t_ + 1 + TT))
                        dc.step(nc.vector.tensor_tensor(xt, xt, ffn1_bias, ALU.add))
                dc.leave()
            dc.settle()

        def product3(out, a, b, first, last_):
            combos = ((a[0], b[0]), (a[0], b[1]), (a[1], b[0]))
            for n, (u, v) in enumerate(combos):
                r = nc.tensor.matmul(out, u, v, start=(first and n == 0), stop=(last_ and n == 2))
            return r

        def pe_stage3(pe):
            prep_pe(pe, 3, 4)
            pe.wait_ge(sig("low34_ready"), 3)
            wh, wl = w34("w1", D)
            with pe.Fori(0, PAIRS) as i:
                for par in range(2):
                    front_done(pe, i, par, 3)
                    for t_ in range(TT):
                        pe.wait_ge(sig("ffn1_added"), at(i, par, TT, t_ + 1))
                        rows = slice(t_ * P, (t_ + 1) * P)
                        for k in range(KD):
                            last = product3(psum[:, 2 + t_, :], (xTh[:, par, k, rows], xTl[:, par, k, rows]),
                                            (wh[:, k, :], wl[:, k, :]), k == 0, k == KD - 1)
                        last.then_inc(sig("ffn1_ready"), 1)
                    front_transpose(pe, i, par + 1, 3, 1 - par)

        H2, G2, HD2 = 32, 8, 16
        ST = 4 * HD2
        NU = TT * G2
        HALF = H2 // 2
        cb = view(area_b, 0, [KD, S])
        ch = view(area_b, 4096, [KD, S], F16)
        cl = view(area_b, 6144, [KD, S], F16)
        q_nat = view(area_b, 8192, [TT, D])
        k_nat = view(area_b, 12288, [TT, P])
        q_stack = view(area_b, 14336, [TT * H2, ST], F16).rearrange("p (t h) d -> p t h d", t=TT)
        k_stack = view(area_b, 22528, [TT * G2 * 2, ST], F16).rearrange("p (t g r) d -> p t g r d", t=TT, g=G2)
        qT4 = view(area_b, 26624, [H2 // 2, S], F16)
        kT4 = view(area_b, 34816, [G2, S], F16)
        o_nat = view(area_b, 38912, [D])
        oT4 = view(area_b, 40960, [KD, P])
        v_one = view(area_b, 43008, [TT * G2, HD2 + 1]).rearrange("p (t g) d -> p t g d", t=TT)
        pT4 = view(area_a, 0, [2, 1024])
        mask_add = view(area_a, 16384, [TT, S], BF16)
        mask_or = view(area_a, 17408, [TT, S], U8)
        mask_q = view(area_a, 17920, [TT, S], U8)
        mask_b = view(area_a, 18432, [B, S], U8)
        b2_q = view(area_a, 20480, [D])
        b2_kv = view(area_a, 22528, [2 * P])
        b2_o = view(area_a, 23552, [D])
        max4 = view(area_a, 25632, [2, 4], BF16)
        minus_ident = view(area_a, 28928, [P], BF16)
        rsum4 = view(area_a, 25664, [2, HALF])
        square_junk4 = view(area_a, 26624, [D])
        identh = view(area_a, 28672, [P], F16)

        def sp_stage4(sp):
            sp.wait_ge(sig("low34_ready"), 3)
            sp.dma_start(mask_q, t["mask_q"].rearrange("(t p) k -> p t k", p=P)).then_inc(sig("tables_loaded"), 16)
            sp.dma_start(mask_b, t["mask_b"].partition_broadcast(P)).then_inc(sig("tables_loaded"), 16)
            for dst, name in ((b2_q, "b2_q"), (b2_kv, "b2_kv"), (b2_o, "b2_o")):
                sp.dma_start(dst, row(name)).then_inc(sig("tables_loaded"), 16)
            sp.sem_inc(sig("ctx4_low_ready"), 1)
            sp.sem_inc(sig("kv4_drained"), TT)
            sp.sem_inc(sig("x4_added"), 1)
            with sp.Fori(0, PAIRS) as i:
                for par in range(2):
                    sp.wait_ge(sig("ctx4_low_ready"), at(i, par, 1, 1))
                    sp.dma_start(cb, t["ctxT"][:, :, i * 2 + par, :]).then_inc(sig("ctx4_loaded"), 16)

        def pool_stage4(pool, pc):
            pool.wait_ge(sig("bound_squares_ready"), 1)
            nc.gpsimd.tensor_tensor(part[:, 12:14], part[:, 10:12], half_pow[:, 0:2], ALU.pow).then_inc(sig("bound_roots_ready"), 1)
            with pool.Fori(0, PAIRS) as i:
                pc.enter(i, 2, PAIRS)
                for par in range(2):
                    front_rstd(pool, pc, i, par + 1, 4)
                pc.leave()

        def pe_stage4(pe):
            wqh, wql = w34("w2_q", D)
            wkh, wkl = w34("w2_kv", 2 * P)
            pe.wait_ge(sig("ffn1_added"), TT * B + TT)

            def half16(bank):
                return psum[:, bank, :].bitcast(F16).rearrange("p (n q) -> p n q", q=P)

            def scores(i, par, u):
                t_, g = divmod(u, G2)
                if u >= 1:
                    pe.wait_ge(sig("max4_ready"), at(i, par, NU, u))
                for hh in range(4):
                    v, hp = hh % 2, hh // 2
                    out = psum[:, 2 + v, hp * S:(hp + 1) * S]
                    rows = slice(ST * v, ST * v + ST)
                    nc.tensor.matmul(out, identb[:, :], mask_add[:, t_, :], start=True, stop=False)
                    last = nc.tensor.matmul(out, qT4[rows, 2 * g + hp, t_ * P:(t_ + 1) * P], kT4[rows, g, :], start=False, stop=True)
                last.then_inc(sig("s4_ready"), 1)

            def scores_T(i, par, u):
                t_, g = divmod(u, G2)
                pe.wait_ge(sig("max4_ready"), at(i, par, NU, u + 1))
                if u >= 2:
                    pe.wait_ge(sig("p4_ready"), at(i, par, NU, u - 1))
                for v in range(2):
                    rows = slice(ST * v, ST * v + ST)
                    for k in range(TT):
                        out = psum[:, 4 + 2 * (u % 2) + v, k * S:(k + 1) * S]
                        keys = slice(k * P, (k + 1) * P)
                        nc.tensor.matmul(out.rearrange("p (h q) -> p h q", h=2), mask_add[:, t_, keys],
                                         identb[:, :].unsqueeze(1).broadcast_to([P, 2, P]), start=True, stop=False)
                        for hp in range(2):
                            nc.tensor.matmul(out[:, hp * P:(hp + 1) * P],
                                             max4[:, u % 2, 2 * v + hp:2 * v + hp + 1].broadcast_to([P, P]), minus_ident,
                                             start=False, stop=False)
                        last = nc.tensor.matmul(out.rearrange("p (h q) -> p h q", h=2), kT4[rows, g, keys],
                                                qT4[rows, 2 * g:2 * g + 2, t_ * P:(t_ + 1) * P], start=False, stop=True)
                last.then_inc(sig("sT4_ready"), 1)

            def values(i, par, u):
                t_, g = divmod(u, G2)
                if g == 0:
                    pe.wait_ge(sig("x4_added"), at(i, par, TT, t_ + 1))
                if g == G2 // 2:
                    pe.wait_ge(sig("o4_nat_ready"), at(i, par, 2 * TT, 2 * t_ + 1))
                pe.wait_ge(sig("p4_ready"), at(i, par, NU, u + 1))
                for hh in range(4):
                    v, hp = hh % 2, hh // 2
                    h = (4 * g + hh) % HALF
                    for k in range(TT):
                        n = (v * TT + k) * 2 + hp
                        last = nc.tensor.matmul(psum[:, 1, h * (HD2 + 1):(h + 1) * (HD2 + 1)], pT4[:, u % 2, n * P:(n + 1) * P],
                                                v_one[:, k, g, :], start=(k == 0), stop=(k == TT - 1))
                if g % 4 == 3:
                    last.then_inc(sig("o4_ready"), 1)
                if g == G2 - 1:
                    pe.wait_ge(sig("o4_nat_ready"), at(i, par, 2 * TT, 2 * t_ + 2))
                    for k in range(KD):
                        last = nc.tensor.transpose(psum[:, 1, k * P:(k + 1) * P], o_nat[:, k * P:(k + 1) * P], ident[:, :])
                    last.then_inc(sig("oT4_ps_ready"), 1)
                    pe.wait_ge(sig("oT4_ready"), at(i, par, TT, t_ + 1))
                    for k in range(KD):
                        last = nc.tensor.matmul(psum[:, 1, :], oT4[:, k, :], w2_o[:, k, :], start=(k == 0), stop=(k == KD - 1))
                    last.then_inc(sig("y4_ready"), 1)

            with pe.Fori(0, PAIRS) as i:
                for par in range(2):
                    front_done(pe, i, par, 4)
                    for t_ in range(TT):
                        rows = slice(t_ * P, (t_ + 1) * P)
                        for k in range(KD):
                            last = product3(psum[:, 2 + t_, :], (xTh[:, par, k, rows], xTl[:, par, k, rows]),
                                            (wqh[:, k, :], wql[:, k, :]), k == 0, k == KD - 1)
                        last.then_inc(sig("q4_ps_ready"), 1)
                    pe.wait_ge(sig("ctx4_low_ready"), at(i, par, 1, 2))
                    for t_ in range(TT):
                        rows = slice(t_ * P, (t_ + 1) * P)
                        for k in range(KD):
                            last = product3(psum[:, 4 + t_, 0:2 * P], (ch[:, k, rows], cl[:, k, rows]),
                                            (wkh[:, k, :], wkl[:, k, :]), k == 0, k == KD - 1)
                        last.then_inc(sig("kv4_ps_ready"), 1)
                    front_transpose(pe, i, par + 1, 4, 1 - par)
                    for t_ in range(TT):
                        pe.wait_ge(sig("q4_stacked"), at(i, par, TT, t_ + 1))
                        for n in range(2):
                            if t_ == 1:
                                pe.wait_ge(sig("qT4_ready"), at(i, par, 2 * TT, n + 1))
                            for m in range(8):
                                c = 8 * n + m
                                last = nc.tensor.transpose(half16(6 + n)[:, m, :], q_stack[:, t_, 2 * c:2 * c + 2, :].rearrange("p h d -> p (h d)"), identh)
                            last.then_inc(sig("qT4_ps_ready"), 1)
                    for t_ in range(TT):
                        pe.wait_ge(sig("k4_stacked"), at(i, par, TT, t_ + 1))
                        pe.wait_ge(sig("kv4_drained"), at(i, par, TT, 2 * TT))
                        for g in range(G2):
                            last = nc.tensor.transpose(half16(4 + t_)[:, g, :], k_stack[:, t_, g].rearrange("p r d -> p (r d)"), identh)
                        last.then_inc(sig("kT4_ps_ready"), 1)
                    pe.wait_ge(sig("qT4_ready"), at(i, par, 2 * TT, 2 * TT))
                    pe.wait_ge(sig("kT4_ready"), at(i, par, TT, TT))
                    pe.wait_ge(sig("mask_ready"), at(i, par, TT, TT))
                    scores(i, par, 0)
                    for u in range(NU):
                        if u + 1 < NU:
                            scores(i, par, u + 1)
                        scores_T(i, par, u)
                        if u >= 1:
                            values(i, par, u - 1)
                    values(i, par, NU - 1)

        def act_stage4(act):
            act.wait_ge(sig("tables_loaded"), 80)
            for n, (b_, w) in enumerate(((b2_q, D), (b2_kv, 2 * P))):
                nc.scalar.activation(square_junk4[:, 0:w], b_, ACT.Square, accum_out=part[:, 8 + n:9 + n]).then_inc(sig("bound_sums_ready"), 1)
                act.wait_ge(sig("bound_sums_ready"), n + 1)
            act.wait_ge(sig("scales4_ready"), 1)
            with act.Fori(0, PAIRS) as i:
                for par in range(2):
                    act.wait_ge(sig("ctx4_loaded"), i * 32 + (par * 16 + 16))
                    act.wait_ge(sig("kv4_drained"), at(i, par, TT, TT))
                    nc.scalar.activation(ch, cb, ACT.Copy, scale=S1("s_ctx")).then_inc(sig("ctx4_high_ready"), 1)
                    for t_ in range(TT):
                        act.wait_ge(sig("q4_nat_ready"), at(i, par, TT, t_ + 1))
                        src = q_nat[:, t_, :].rearrange("p (h d) -> p h d", h=H2)
                        for slot in range(2):
                            nc.scalar.activation(q_stack[:, t_, :, slot * HD2:(slot + 1) * HD2], src, ACT.Copy).then_inc(sig("q4_high_ready"), 1)
                    for t_ in range(TT):
                        act.wait_ge(sig("k4_nat_ready"), at(i, par, TT, t_ + 1))
                        src = k_nat[:, t_, :].rearrange("p (g d) -> p g d", g=G2).unsqueeze(2).broadcast_to([P, G2, 2, HD2])
                        for slot in (0, 2):
                            nc.scalar.activation(k_stack[:, t_, :, :, slot * HD2:(slot + 1) * HD2], src, ACT.Copy).then_inc(sig("k4_high_ready"), 1)
                    front_high(act, i, par + 1, 4, 1 - par)
                    for t_ in range(TT):
                        for n in range(2):
                            act.wait_ge(sig("qT4_ps_ready"), at(i, par, 2 * TT, 2 * t_ + n + 1))
                            nc.scalar.activation(qT4[:, 8 * n:8 * n + 8, t_ * P:(t_ + 1) * P],
                                                 psum[:, 6 + n, :].bitcast(F16).rearrange("p (n q) -> p n q", q=P),
                                                 ACT.Copy).then_inc(sig("qT4_ready"), 1)
                    for t_ in range(TT):
                        act.wait_ge(sig("kT4_ps_ready"), at(i, par, TT, t_ + 1))
                        nc.scalar.activation(kT4[:, :, t_ * P:(t_ + 1) * P],
                                             psum[:, 4 + t_, :].bitcast(F16).rearrange("p (n q) -> p n q", q=P), ACT.Copy).then_inc(sig("kT4_ready"), 1)
                    for u in range(NU + 1):
                        if u < NU:
                            act.wait_ge(sig("sT4_ready"), at(i, par, NU, u + 1))
                            src = psum[:, 4 + 2 * (u % 2):6 + 2 * (u % 2), :].rearrange("p a n -> p (a n)")
                            nc.scalar.activation(pT4[:, u % 2, :], src, ACT.Exp, scale=S1("exp4")).then_inc(sig("p4_ready"), 1)
                        if u >= 1 and (u - 1) % G2 == G2 - 1:
                            t_ = (u - 1) // G2
                            act.wait_ge(sig("oT4_ps_ready"), at(i, par, TT, t_ + 1))
                            nc.scalar.activation(oT4, psum[:, 1, :].rearrange("p (k n) -> p k n", k=KD),
                                                 ACT.Copy).then_inc(sig("oT4_ready"), 1)

        def dve_stage4(dve, dc):
            dve.wait_ge(sig("tables_loaded"), 80)
            dve.wait_ge(sig("bound_sums_ready"), 2)
            nc.vector.tensor_scalar(part[:, 10:12], part[:, 8:10], 1e-30, None, ALU.max).then_inc(sig("bound_squares_ready"), 1)
            dc.step(nc.vector.tensor_copy(identh, ident[:, :]))
            dc.step(nc.vector.memset(q_stack[:, :, :, 3 * HD2:ST], 0.0))
            dc.step(nc.vector.memset(k_stack[:, :, :, :, 3 * HD2:ST], 0.0))
            dc.step(nc.vector.memset(v_one[:, :, :, HD2:HD2 + 1], 1.0))
            dc.step(nc.vector.tensor_scalar(b2_o, b2_o, gates[:, 2:3], None, ALU.mult))
            dc.step(nc.vector.tensor_scalar(S1("q4"), S1("inv_w2_q"), 1.0 / LN_SCALE, None, ALU.mult))
            dc.step(nc.vector.tensor_tensor(S1("kv4"), S1("inv_w2_kv"), S1("inv_ctx"), ALU.mult))
            dve.wait_ge(sig("bound_roots_ready"), 1)
            dc.settle()
            dc.step(nc.vector.tensor_tensor(part[:, 12:14], part[:, 12:14], part[:, 10:12], ALU.mult))
            dc.settle()
            dc.step(nc.vector.scalar_tensor_tensor(out=part[:, 14:15], in0=S1("inv_w2_q"), scalar=NORM * math.sqrt(D),
                                                   in1=part[:, 12:13], op0=ALU.mult, op1=ALU.add))
            dc.step(nc.vector.scalar_tensor_tensor(out=part[:, 15:16], in0=S1("kv4"), scalar=NORM * NORM,
                                                   in1=part[:, 13:14], op0=ALU.mult, op1=ALU.add))
            dc.settle()
            dc.link(nc.vector.tensor_scalar(part[:, 14:16], part[:, 14:16], 1.0 / NORM, 1e-30, ALU.mult, ALU.max))
            dc.step(nc.vector.scalar_tensor_tensor(out=S1("exp4"), in0=part[:, 14:15], scalar=HD2 ** -0.5, in1=part[:, 15:16],
                                                   op0=ALU.mult, op1=ALU.mult))
            dc.link(nc.vector.reciprocal(part[:, 12:14], part[:, 14:16]))
            dc.step(nc.vector.tensor_tensor(S1("q4"), S1("q4"), part[:, 12:13], ALU.mult))
            dc.step(nc.vector.tensor_tensor(S1("k4"), S1("kv4"), part[:, 13:14], ALU.mult))
            dc.step(nc.vector.tensor_scalar(b2_q, b2_q, part[:, 12:13], None, ALU.mult))
            dc.step(nc.vector.tensor_scalar(b2_kv[:, 0:P], b2_kv[:, 0:P], part[:, 13:14], None, ALU.mult))
            dc.settle()
            nc.vector.tensor_scalar(minus_ident, ident[:, :], -1.0, None, ALU.mult).then_inc(sig("scales4_ready"), 1)
            with dve.Fori(0, PAIRS) as i:
                dc.enter(i, 20, PAIRS)
                for par in range(2):
                    dve.wait_ge(sig("ctx4_high_ready"), at(i, par, 1, 1))
                    nc.vector.scalar_tensor_tensor(out=cl, in0=cb, scalar=S1("s_ctx"), in1=ch, op0=ALU.mult,
                                                   op1=ALU.subtract).then_inc(sig("ctx4_low_ready"), 1)
                    pad = mask_b[:, i * 2 + par, :]
                    for t_ in range(TT):
                        dc.step(nc.vector.tensor_tensor(mask_or[:, t_, :], mask_q[:, t_, :], pad, ALU.max))
                    dc.settle()
                    for t_ in range(TT):
                        nc.vector.tensor_scalar(mask_add[:, t_, :], mask_or[:, t_, :], NEG, None, ALU.mult).then_inc(sig("mask_ready"), 1)
                    for t_ in range(TT):
                        dve.wait_ge(sig("q4_ps_ready"), at(i, par, TT, t_ + 1))
                        nc.vector.scalar_tensor_tensor(out=q_nat[:, t_, :], in0=psum[:, 2 + t_, :], scalar=S1("q4"), in1=b2_q,
                                                       op0=ALU.mult, op1=ALU.add).then_inc(sig("q4_nat_ready"), 1)
                    for t_ in range(TT):
                        dve.wait_ge(sig("kv4_ps_ready"), at(i, par, TT, t_ + 1))
                        nc.vector.scalar_tensor_tensor(out=k_nat[:, t_, :], in0=psum[:, 4 + t_, 0:P], scalar=S1("k4"), in1=b2_kv[:, 0:P],
                                                       op0=ALU.mult, op1=ALU.add).then_inc(sig("k4_nat_ready"), 1)
                        nc.vector.scalar_tensor_tensor(out=v_one[:, t_, :, 0:HD2], in0=psum[:, 4 + t_, P:2 * P].rearrange("p (g d) -> p g d", g=G2),
                                                       scalar=S1("kv4"), in1=b2_kv[:, P:2 * P].rearrange("p (g d) -> p g d", g=G2),
                                                       op0=ALU.mult, op1=ALU.add).then_inc(sig("kv4_drained"), 1)
                    for t_ in range(TT):
                        dve.wait_ge(sig("q4_high_ready"), at(i, par, 2 * TT, 2 * t_ + 2))
                        nc.vector.tensor_tensor(q_stack[:, t_, :, 2 * HD2:3 * HD2], q_nat[:, t_, :].rearrange("p (h d) -> p h d", h=H2),
                                                q_stack[:, t_, :, 0:HD2], ALU.subtract).then_inc(sig("q4_stacked"), 1)
                    for t_ in range(TT):
                        dve.wait_ge(sig("k4_high_ready"), at(i, par, 2 * TT, 2 * t_ + 2))
                        src = k_nat[:, t_, :].rearrange("p (g d) -> p g d", g=G2).unsqueeze(2).broadcast_to([P, G2, 2, HD2])
                        nc.vector.tensor_tensor(k_stack[:, t_, :, :, HD2:2 * HD2], src, k_stack[:, t_, :, :, 0:HD2],
                                                ALU.subtract).then_inc(sig("k4_stacked"), 1)
                    front_norm(dve, dc, i, par + 1, 4, following(i, par), 1 - par)
                    front_low(dve, i, par + 1, 4, 1 - par)
                    for u in range(NU + 2):
                        if u < NU:
                            dve.wait_ge(sig("s4_ready"), at(i, par, NU, u + 1))
                            src = psum[:, 2:4, :].rearrange("p a (h k) -> p (a h) k", h=2)
                            nc.vector.reduce_max(max4[:, u % 2, :], src, AX.X).then_inc(sig("max4_ready"), 1)
                        if u >= 2 and (u - 2) % 4 == 3:
                            t_, g = divmod(u - 2, G2)
                            hf = g // 4
                            src = psum[:, 1, 0:HALF * (HD2 + 1)].rearrange("p (h d) -> p h d", h=HALF)
                            dve.wait_ge(sig("o4_ready"), at(i, par, 2 * TT, 2 * t_ + hf + 1))
                            dc.link(nc.vector.reciprocal(rsum4[:, hf, :], src[:, :, HD2]))
                            nc.vector.tensor_tensor(o_nat[:, hf * 256:(hf + 1) * 256].rearrange("p (h d) -> p h d", h=HALF),
                                                    src[:, :, 0:HD2], rsum4[:, hf, :].unsqueeze(2).broadcast_to([P, HALF, HD2]),
                                                    ALU.mult).then_inc(sig("o4_nat_ready"), 1)
                            if hf == 1:
                                xt = X[:, (i * 2 + par) * TT + t_, :]
                                dve.wait_ge(sig("y4_ready"), at(i, par, TT, t_ + 1))
                                nc.vector.scalar_tensor_tensor(out=xt, in0=psum[:, 1, :], scalar=gates[:, 2:3], in1=xt,
                                                               op0=ALU.mult, op1=ALU.add).then_inc(sig("x4_added"), 1)
                                dve.wait_ge(sig("x4_added"), at(i, par, TT, t_ + 2))
                                dc.step(nc.vector.tensor_tensor(xt, xt, b2_o, ALU.add))
                dc.leave()
            dc.settle()
            dve.sem_inc(sig("stage_done"), 1)

        TOPK = int(E * (1.0 - 0.9))
        HALVINGS = 26
        prep5 = add_prep(5, [("w2_syn", 8, "ternary", flat(area_b, 0, 8192), None),
                             ("w2_out", 8, "ternary", flat(area_b, 16384, 8192), None)])
        w5_syn = view(area_b, 0, [KD, E], F16)
        w5_out = view(area_b, 16384, [KE, D], F16)
        z5 = view(area_a, 0, [TT, E])
        h5h = [view(area_a, 16384, [KE, P], F16), view(area_c, 0, [KE, P], F16)]
        h5l = [view(area_a, 20480, [KE, P], F16), view(area_c, 4096, [KE, P], F16)]
        b5_syn = view(area_a, 24576, [E])
        b5_out = view(area_a, 32768, [D])
        gamma5 = view(area_a, 34816, [D])
        beta5 = view(area_a, 36864, [D])
        y5 = view(area_a, 38912, [D])
        junk5 = view(area_g, 0, [TT, E], F16)
        halves = view(area_g, 8192, [TT, HALVINGS])
        lows5 = view(area_g, 8448, [2, TT])
        lo5 = lows5[:, HALVINGS % 2, :]
        cand5 = view(area_g, 8528, [TT])
        count5 = view(area_g, 8496, [TT])
        take5 = view(area_g, 8512, [TT])
        ENOUGH = (TOPK - 0.5, E + 1.5 - 2.0 * TOPK)
        max5 = view(area_g, 8544, [TT])
        pow2 = view(area_g, 8576, [HALVINGS])

        def sp_stage5(sp):
            sp.wait_ge(sig("stage_done"), 1)
            for dst, name in ((b5_syn, "b2_syn"), (b5_out, "b2_out"), (gamma5, "gamma"), (beta5, "beta")):
                sp.dma_start(dst, row(name)).then_inc(sig("tables_loaded"), 16)
            prep_load(sp, prep5)
            sp.sem_inc(sig("z5_ready"), 4)
            sp.sem_inc(sig("y5_drained"), 1)

        def pool_stage5(pool, pc):
            pool.wait_ge(sig("bound_squares_ready"), 2)
            nc.gpsimd.tensor_tensor(part[:, 29:30], part[:, 28:29], half_pow[:, 0:1], ALU.pow).then_inc(sig("bound_roots_ready"), 1)
            with pool.Fori(0, PAIRS) as i:
                pc.enter(i, 6, PAIRS)
                for par in range(2):
                    front_rstd(pool, pc, i, par + 1, 5)
                    for t_ in range(TT):
                        pool.wait_ge(sig("stats5_ready"), at(i, par, TT, t_ + 1))
                        pc.link(nc.gpsimd.tensor_tensor(rstd5, mv5[:, 1:2], eps_col[:, 0:1], ALU.add))
                        nc.gpsimd.tensor_tensor(rstd5, rstd5, half_pow[:, 0:1], ALU.pow).then_inc(sig("rstd5_ready"), 1)
                pc.leave()

        stats5 = view(area_g, 8704, [6])
        mv5 = view(area_g, 8736, [2])
        rstd5 = view(area_g, 8752, [1])

        def pe_stage5(pe):
            prep_pe(pe, 5, 2)
            pe.wait_ge(sig("weights_ready"), 2)
            with pe.Fori(0, PAIRS) as i:
                for par in range(2):
                    front_done(pe, i, par, 5)
                    for t_ in range(TT):
                        for n in range(4):
                            if n == 0 or t_ == 1:
                                pe.wait_ge(sig("z5_ready") if t_ else sig("h5_low_ready5"), at(i, par, 4 * TT, 4 + n + 1) if t_ else at(i, par, 4 * TT, 1))
                            for k in range(KD):
                                for m, xt in enumerate((xTh, xTl)):
                                    last = nc.tensor.matmul(psum[:, 2 + n, :], xt[:, par, k, t_ * P:(t_ + 1) * P],
                                                            w5_syn[:, k, n * 512:(n + 1) * 512], start=(k == 0 and m == 0),
                                                            stop=(k == KD - 1 and m == 1))
                            last.then_inc(sig("z5_ps_ready"), 1)
                    for t_ in range(TT):
                        pe.wait_ge(sig("hid5_ready"), at(i, par, TT, t_ + 1))
                        for n in range(4):
                            if t_ == 1:
                                pe.wait_ge(sig("h5_low_ready5"), at(i, par, 4 * TT, n + 2))
                            for m in range(4):
                                k = 4 * n + m
                                last = nc.tensor.transpose(psum[:, 2 + n, m * P:(m + 1) * P], z5[:, t_, k * P:(k + 1) * P], ident[:, :])
                            last.then_inc(sig("h5_ps_ready"), 1)
                    front_transpose(pe, i, par + 1, 5, 1 - par)
                    for t_ in range(TT):
                        pe.wait_ge(sig("y5_drained"), at(i, par, TT, t_ + 1))
                        for n in range(4):
                            pe.wait_ge(sig("h5_low_ready5"), at(i, par, 4 * TT, 4 * t_ + n + 2))
                            for k in range(4 * n, 4 * n + 4):
                                for m, h in enumerate((h5h[t_], h5l[t_])):
                                    last = nc.tensor.matmul(psum[:, 6, :], h[:, k, :], w5_out[:, k, :], start=(k == 0 and m == 0),
                                                            stop=(k == KE - 1 and m == 1))
                        last.then_inc(sig("y5_ready"), 1)

        def act_stage5(act):
            act.wait_ge(sig("tables_loaded"), 144)
            act.wait_ge(sig("weights5_tables"), 1)
            nc.scalar.activation(z5[:, 0, :], b5_syn, ACT.Square, accum_out=part[:, 27:28]).then_inc(sig("bound_sums_ready"), 1)
            prep_act(act, prep5, 5, None)
            with act.Fori(0, PAIRS) as i:
                for par in range(2):
                    for k in range(HALVINGS):
                        act.wait_ge(sig("cand5_ready"), at(i, par, HALVINGS, k + 1))
                        nc.scalar.activation(junk5[:, 1, :], z5[:, 1, :], ACT.Sign, bias=cand5[:, 1:2], scale=-1.0,
                                             accum_out=count5[:, 1:2]).then_inc(sig("count5_ready"), 1)
                    for t_ in range(TT):
                        for n in range(4):
                            act.wait_ge(sig("h5_ps_ready"), at(i, par, 4 * TT, 4 * t_ + n + 1))
                            nc.scalar.activation(h5h[t_][:, 4 * n:4 * n + 4, :], psum[:, 2 + n, :].rearrange("p (k q) -> p k q", k=4),
                                                 ACT.Copy, scale=S1("k5")).then_inc(sig("h5_high_ready"), 1)
                    front_high(act, i, par + 1, 5, 1 - par)

        def dve_stage5(dve, dc):
            dve.wait_ge(sig("x4_added"), TT * B + 1)
            dve.wait_ge(sig("tables_loaded"), 144)
            nc.vector.tensor_copy(part[:, 30:31], part[:, 31:32]).then_inc(sig("weights5_tables"), 1)
            prep_dve(dve, dc, prep5, 5, None)
            dve.wait_ge(sig("bound_sums_ready"), 3)
            nc.vector.tensor_scalar(part[:, 28:29], part[:, 27:28], 1e-30, None, ALU.max).then_inc(sig("bound_squares_ready"), 1)
            dc.step(nc.vector.tensor_scalar(b5_out, b5_out, 1.0, None, ALU.mult))
            dc.step(nc.vector.tensor_scalar(gamma5, gamma5, gates[:, 6:7], None, ALU.mult))
            dc.step(nc.vector.tensor_scalar(beta5, beta5, gates[:, 6:7], None, ALU.mult))
            for k in range(HALVINGS):
                dc.step(nc.vector.memset(pow2[:, k:k + 1], 2.0 ** -(k + 1)))
            dve.wait_ge(sig("bound_roots_ready"), 2)
            dc.settle()
            dc.step(nc.vector.tensor_tensor(part[:, 30:31], part[:, 28:29], part[:, 29:30], ALU.mult))
            dc.step(nc.vector.tensor_scalar(S1("z5"), S1("mean_w2_syn"), 1.0 / LN_SCALE, None, ALU.mult))
            dc.settle()
            dc.link(nc.vector.scalar_tensor_tensor(out=part[:, 31:32], in0=S1("mean_w2_syn"), scalar=float(D), in1=part[:, 30:31],
                                                   op0=ALU.mult, op1=ALU.add))
            dc.link(nc.vector.tensor_scalar(part[:, 31:32], part[:, 31:32], 1.0 / NORM, 1e-30, ALU.mult, ALU.max))
            dc.step(nc.vector.reciprocal(S1("k5"), part[:, 31:32]))
            dc.step(nc.vector.tensor_tensor(S1("y5"), part[:, 31:32], S1("mean_w2_out"), ALU.mult))
            dc.settle()
            dve.wait_ge(sig("stage_free"), len(plan5))
            nc.vector.tensor_copy(part[:, 30:31], S1("k5")).then_inc(sig("weights_ready"), 1)
            nc.vector.tensor_copy(part[:, 29:30], S1("k5")).then_inc(sig("h5_low_ready5"), 1)
            with dve.Fori(0, PAIRS) as i:
                dc.enter(i, 294, PAIRS)
                for par in range(2):
                    for t_ in range(TT):
                        for n in range(4):
                            dve.wait_ge(sig("z5_ps_ready"), at(i, par, 4 * TT, 4 * t_ + n + 1))
                            nc.vector.scalar_tensor_tensor(out=z5[:, t_, n * 512:(n + 1) * 512], in0=psum[:, 2 + n, :], scalar=S1("z5"),
                                                           in1=b5_syn[:, n * 512:(n + 1) * 512], op0=ALU.mult,
                                                           op1=ALU.add).then_inc(sig("z5_ready"), 1)
                    front_norm(dve, dc, i, par + 1, 5, following(i, par), 1 - par)
                    dve.wait_ge(sig("z5_ready"), at(i, par, 4 * TT, 4 * TT + 4))
                    dc.link(nc.vector.reduce_max(max5, z5, AX.X))
                    dc.step(nc.vector.memset(lows5[:, 0, :], 0.0))
                    for t_ in range(TT):
                        dc.step(nc.vector.tensor_scalar(halves[:, t_, :], pow2, max5[:, t_:t_ + 1], 0.0, ALU.mult, ALU.max))
                    dc.settle()
                    nc.vector.tensor_copy(cand5, halves[:, :, 0]).then_inc(sig("cand5_ready"), 1)
                    for k in range(HALVINGS):
                        dve.wait_ge(sig("cand5_ready"), at(i, par, HALVINGS, k + 1))
                        dc.step(nc.vector.tensor_scalar(junk5[:, 0, :], z5[:, 0, :], cand5[:, 0:1], 0.0, ALU.is_ge, ALU.add,
                                                        accum_out=count5[:, 0:1]))
                        dve.wait_ge(sig("count5_ready"), at(i, par, HALVINGS, k + 1))
                        dc.settle()
                        for t_ in range(TT):
                            dc.step(nc.vector.scalar_tensor_tensor(out=take5[:, t_:t_ + 1], in0=count5[:, t_:t_ + 1], scalar=ENOUGH[t_],
                                                                   in1=cand5[:, t_:t_ + 1], op0=(ALU.is_gt, ALU.is_lt)[t_], op1=ALU.mult))
                        dc.settle()
                        if k + 1 < HALVINGS:
                            for t_ in range(TT):
                                r = nc.vector.scalar_tensor_tensor(out=cand5[:, t_:t_ + 1], in0=take5[:, t_:t_ + 1], scalar=lows5[:, k % 2, t_:t_ + 1],
                                                                   in1=halves[:, t_, k + 1:k + 2], op0=ALU.max, op1=ALU.add)
                                if t_ == 0:
                                    dc.step(r)
                                else:
                                    r.then_inc(sig("cand5_ready"), 1)
                        dc.step(nc.vector.tensor_tensor(lows5[:, (k + 1) % 2, :], lows5[:, k % 2, :], take5, ALU.max))
                    dc.settle()
                    for t_ in range(TT):
                        nc.vector.scalar_tensor_tensor(out=z5[:, t_, :], in0=z5[:, t_, :], scalar=lo5[:, t_:t_ + 1], in1=z5[:, t_, :],
                                                       op0=ALU.is_ge, op1=ALU.mult).then_inc(sig("hid5_ready"), 1)
                    for t_ in range(TT):
                        for n in range(4):
                            dve.wait_ge(sig("h5_high_ready"), at(i, par, 4 * TT, 4 * t_ + n + 1))
                            nc.vector.scalar_tensor_tensor(out=h5l[t_][:, 4 * n:4 * n + 4, :],
                                                           in0=psum[:, 2 + n, :].rearrange("p (k q) -> p k q", k=4), scalar=S1("k5"),
                                                           in1=h5h[t_][:, 4 * n:4 * n + 4, :], op0=ALU.mult,
                                                           op1=ALU.subtract).then_inc(sig("h5_low_ready5"), 1)
                    front_low(dve, i, par + 1, 5, 1 - par)
                    for t_ in range(TT):
                        dve.wait_ge(sig("y5_ready"), at(i, par, TT, t_ + 1))
                        nc.vector.scalar_tensor_tensor(out=y5, in0=psum[:, 6, :], scalar=S1("y5"), in1=xn[:, par, t_, :], op0=ALU.mult,
                                                       op1=ALU.add).then_inc(sig("y5_drained"), 1)
                        dve.wait_ge(sig("y5_drained"), at(i, par, TT, t_ + 2))
                        dc.link(nc.vector.tensor_tensor(y5, y5, b5_out, ALU.add))
                        dc.link(nc.vector.bn_stats(stats5, y5))
                        dve.sem_inc(sig("stats_seen"), 1)
                        nc.vector.bn_aggr(mv5, stats5).then_inc(sig("stats5_ready"), 1)
                        dve.wait_ge(sig("rstd5_ready"), at(i, par, TT, t_ + 1))
                        dc.link(nc.vector.tensor_scalar(y5, y5, mv5[:, 0:1], rstd5, ALU.subtract, ALU.mult))
                        dc.link(nc.vector.tensor_tensor(y5, y5, gamma5, ALU.mult))
                        dc.link(nc.vector.tensor_tensor(y5, y5, beta5, ALU.add))
                        xt = X[:, (i * 2 + par) * TT + t_, :]
                        dc.link(nc.vector.tensor_tensor(xt, xt, y5, ALU.add))
                dc.leave()
            dc.settle()
            dve.sem_inc(sig("stage_done"), 1)

        plan5 = list(plan)

        H3, G3 = 16, 4
        prep6 = add_prep(6, [("w3_q", 8, "split", flat(area_a, 0, 8192), flat(area_a, 16384, 8192)),
                             ("w3_k", 2, "split", flat(area_a, 32768, 2048), flat(area_a, 36864, 2048)),
                             ("w3_kc", 2, "split", flat(area_a, 40960, 2048), flat(area_a, 45056, 2048)),
                             ("w3_v", 2, "split", flat(area_b, 0, 2048), flat(area_b, 4096, 2048)),
                             ("w3_vc", 2, "split", flat(area_b, 8192, 2048), flat(area_b, 12288, 2048))])
        w6 = {m[0]: [w.rearrange("p (k n) -> p k n", k=KD) for w in (m[3], m[4])] for m in prep6[0]}
        w3_o = view(area_c, 0, [KE, D])
        n6 = view(area_b, 16384, [H3, P])
        r6 = view(area_b, 24576, [H3, P])
        qT6 = view(area_b, 32768, [H3, P])
        kT6 = view(area_b, 40960, [G3, 4 * P])
        v6 = view(area_g, 0, [4, D])
        turn6 = view(area_g, 8192, [H3, P])
        p6 = view(area_g, 8192, [2, 4 * P])
        pT6 = view(area_g, 12288, [2, 4 * P]).rearrange("p a (n q) -> p a n q", n=4)
        rope6 = view(area_g, 16384, [8, P]).rearrange("p (w t c) d -> p w t c d", w=2, t=2)
        cb6 = stage[:, 0, :].rearrange("p (k s) -> p k s", k=KD)
        ch6 = stage[:, 1, 0:512].bitcast(F16).rearrange("p (k s) -> p k s", k=KD)
        cl6 = stage[:, 1, 512:1024].bitcast(F16).rearrange("p (k s) -> p k s", k=KD)
        small6 = sb("small6", [P, 96])
        squares6, root6 = small6[:, 0:H3], small6[:, 16:16 + H3]
        nmax6 = small6[:, 34:36]
        sum6, rsum6 = small6[:, 48:48 + H3], small6[:, 64:64 + H3]
        key_w6 = sb("key_w6", [P, P])
        norm_w6 = view(area_b, 16384, [2, P])
        tri6 = sb("tri6", [P, P], BF16)
        tri_raw = view(area_b, 17408, [P])
        SC6 = float(P) ** -0.5
        NK6 = [3 * P, 4 * P]

        def sp_stage6(sp):
            sp.wait_ge(sig("stage_done"), 2)
            prep_load(sp, prep6)
            sp.dma_start(view(area_c, 0, [8192]), t["w3_o"]).then_inc(sig("tables_loaded"), 16)
            sp.dma_start(norm_w6[:, 0, :], row("qn_w")).then_inc(sig("tables_loaded"), 16)
            sp.dma_start(norm_w6[:, 1, :], row("kn_w")).then_inc(sig("tables_loaded"), 16)
            sp.dma_start(tri_raw, t["c_tri"]).then_inc(sig("tables_loaded"), 16)
            sp.dma_start(rope6[:, 0], t["c_rope"]).then_inc(sig("tables_loaded"), 16)
            sp.dma_start(rope6[:, 1], t["c_rope"]).then_inc(sig("tables_loaded"), 16)
            sp.sem_inc(sig("v6_ready"), 2 * TT)
            sp.sem_inc(sig("x6_added"), 1)
            sp.sem_inc(sig("ctx6_low_ready"), 1)
            sp.wait_ge(sig("weights_ready"), 3)
            with sp.Fori(0, PAIRS) as i:
                for par in range(2):
                    sp.wait_ge(sig("ctx6_low_ready"), at(i, par, 1, 1))
                    sp.dma_start(cb6, t["ctxT"][:, :, i * 2 + par, :]).then_inc(sig("ctx6_loaded"), 16)

        NR6 = 2 * TT

        def pool_stage6(pool, pc):
            prep_pool(pool, 6, 5)
            with pool.Fori(0, PAIRS) as i:
                pc.enter(i, 2, PAIRS)
                for par in range(2):
                    for r in range(NR6):
                        if r == TT:
                            front_rstd(pool, pc, i, par + 1, 6)
                        n = G3 if r < TT else H3
                        wq, t_ = (1, r) if r < TT else (0, r - TT)
                        pool.wait_ge(sig("n6_ready"), at(i, par, NR6, r + 1))
                        tab = rope6[:, wq, t_, 1, :].unsqueeze(1)
                        nc.gpsimd.tensor_tensor(turn6[:, 0:n, 0:64], n6[:, 0:n, 64:P], tab[:, :, 0:64].broadcast_to([P, n, 64]),
                                                ALU.mult).then_inc(sig("turn6_ready"), 1)
                        nc.gpsimd.tensor_tensor(turn6[:, 0:n, 64:P], n6[:, 0:n, 0:64], tab[:, :, 64:P].broadcast_to([P, n, 64]),
                                                ALU.mult).then_inc(sig("turn6_ready"), 1)
                        pool.wait_ge(sig("squares6_ready"), at(i, par, NR6, r + 1))
                        m = 2 * G3 if r < TT else H3
                        nc.gpsimd.tensor_tensor(root6[:, 0:m], squares6[:, 0:m], half_pow[:, 0:m], ALU.pow).then_inc(sig("root6_ready"), 1)
                pc.leave()

        def pe_stage6(pe):
            prep_pe(pe, 6, 5)
            pe.wait_ge(sig("weights_ready"), 3)

            def project(pe, x, name, bank, rows, cols):
                for k in range(KD):
                    last = product3(psum[:, bank, :], (x[0][:, k, rows], x[1][:, k, rows]),
                                    (w6[name][0][:, k, cols], w6[name][1][:, k, cols]), k == 0, k == KD - 1)
                return last

            def scores(i, par, t_, h):
                nk = NK6[t_]
                u = t_ * H3 + h
                if h >= 2:
                    pe.wait_ge(sig("p6_ready"), at(i, par, TT * H3, u - 1))
                nc.tensor.matmul(psum[:, 2 + h % 2, 0:nk], qT6[:, h, :], kT6[:, h // 4, 0:nk], start=True, stop=False)
                nc.tensor.matmul(psum[:, 2 + h % 2, nk - P:nk], identb[:, :], tri6[:, :], start=False, stop=True).then_inc(sig("s6_ready"), 1)

            def transposes(i, par, t_, h):
                u = t_ * H3 + h
                pe.wait_ge(sig("p6_ready"), at(i, par, TT * H3, u + 1))
                if h >= 2:
                    pe.wait_ge(sig("pT6_ready"), at(i, par, TT * H3, u - 1))
                for k in range(NK6[t_] // P):
                    last = nc.tensor.transpose(psum[:, 4 + h % 2, k * P:(k + 1) * P], p6[:, h % 2, k * P:(k + 1) * P], ident[:, :])
                last.then_inc(sig("pT6_ps_ready"), 1)

            def values(i, par, t_, h):
                u = t_ * H3 + h
                pe.wait_ge(sig("pT6_ready"), at(i, par, TT * H3, u + 1))
                if h % 4 == 0 and h >= 8:
                    pe.wait_ge(sig("o6_drained"), at(i, par, 4 * TT, 4 * t_ + h // 4 - 1))
                for k in range(NK6[t_] // P):
                    last = nc.tensor.matmul(psum[:, 6 + (h // 4) % 2, (h % 4) * P:(h % 4 + 1) * P], pT6[:, h % 2, k, :],
                                            v6[:, k, (h // 4) * P:(h // 4 + 1) * P], start=(k == 0), stop=(k == NK6[t_] // P - 1))
                if h % 4 == 3:
                    last.then_inc(sig("o6_ready"), 1)

            with pe.Fori(0, PAIRS) as i:
                for par in range(2):
                    front_done(pe, i, par, 6)
                    pe.wait_ge(sig("ctx6_low_ready"), at(i, par, 1, 2))
                    x = (xTh[:, par], xTl[:, par])
                    for t_ in range(TT):
                        rows = slice(t_ * P, (t_ + 1) * P)
                        every = slice(0, D)
                        if t_ == 1:
                            pe.wait_ge(sig("kT6_ready"), at(i, par, TT, 1))
                            pe.wait_ge(sig("v6_ready"), at(i, par, 2 * TT, 2 + 2 * TT))
                        project(pe, x, "w3_k", 2, rows, every)
                        project(pe, (ch6, cl6), "w3_kc", 3, rows, every).then_inc(sig("k6_ps_ready"), 1)
                        project(pe, x, "w3_v", 4, rows, every)
                        project(pe, (ch6, cl6), "w3_vc", 5, rows, every).then_inc(sig("v6_ps_ready"), 1)
                        pe.wait_ge(sig("r6_ready"), at(i, par, NR6, t_ + 1))
                        for g in range(G3):
                            nc.tensor.transpose(psum[:, 6, g * P:(g + 1) * P], r6[:, g, :], ident[:, :])
                            last = nc.tensor.transpose(psum[:, 7, g * P:(g + 1) * P], r6[:, G3 + g, :], ident[:, :])
                        last.then_inc(sig("kT6_ps_ready"), 1)
                    front_transpose(pe, i, par + 1, 6, 1 - par)
                    pe.wait_ge(sig("v6_ready"), at(i, par, 2 * TT, 4 * TT))
                    for t_ in range(TT):
                        rows = slice(t_ * P, (t_ + 1) * P)
                        for n in range(4):
                            project(pe, x, "w3_q", 2 + n, rows, slice(n * 512, (n + 1) * 512)).then_inc(sig("q6_ps_ready"), 1)
                        pe.wait_ge(sig("r6_ready"), at(i, par, NR6, TT + t_ + 1))
                        for n in range(4):
                            for m in range(4):
                                last = nc.tensor.transpose(psum[:, 2 + n, m * P:(m + 1) * P], r6[:, 4 * n + m, :], ident[:, :])
                            last.then_inc(sig("qT6_ps_ready"), 1)
                        pe.wait_ge(sig("qT6_ready"), at(i, par, 4 * TT, 4 * t_ + 4))
                        pe.wait_ge(sig("kT6_ready"), at(i, par, TT, TT))
                        scores(i, par, t_, 0)
                        for h in range(H3):
                            if h + 1 < H3:
                                scores(i, par, t_, h + 1)
                            transposes(i, par, t_, h)
                            if h >= 1:
                                values(i, par, t_, h - 1)
                        values(i, par, t_, H3 - 1)
                        for n in range(4):
                            pe.wait_ge(sig("o6_drained"), at(i, par, 4 * TT, 4 * t_ + n + 1))
                            for m in range(4):
                                last = nc.tensor.transpose(psum[:, 2 + n, m * P:(m + 1) * P], n6[:, 4 * n + m, :], ident[:, :])
                            last.then_inc(sig("oT6_ps_ready"), 1)
                        pe.wait_ge(sig("x6_added"), at(i, par, TT, t_ + 1))
                        for n in range(4):
                            pe.wait_ge(sig("oT6_ready"), at(i, par, 4 * TT, 4 * t_ + n + 1))
                            for k in range(4 * n, 4 * n + 4):
                                last = nc.tensor.matmul(psum[:, 1, :], r6[:, k, :], w3_o[:, k, :], start=(k == 0), stop=(k == KE - 1))
                        last.then_inc(sig("y6_ready"), 1)

        def act_stage6(act):
            prep_act(act, prep6, 6, None)
            act.wait_ge(sig("weights_ready"), 3)
            with act.Fori(0, PAIRS) as i:
                for par in range(2):
                    act.wait_ge(sig("ctx6_loaded"), i * 32 + (par * 16 + 16))
                    nc.scalar.activation(ch6, cb6, ACT.Copy, scale=S1("s_ctx")).then_inc(sig("ctx6_high_ready"), 1)
                    for t_ in range(TT):
                        act.wait_ge(sig("k6_ps_ready"), at(i, par, TT, t_ + 1))
                        for src, s in ((2, "k6"), (3, "kc6")):
                            nc.scalar.activation(r6[:, 4 * (src - 2):4 * (src - 2) + 4, :], psum[:, src, :].rearrange("p (h d) -> p h d", h=4),
                                                 ACT.Square, scale=S1(s)).then_inc(sig("sq6_ready"), 1)
                        for src, s in ((2, "k6"), (3, "kc6")):
                            last = nc.scalar.activation(n6[:, 4 * (src - 2):4 * (src - 2) + 4, :],
                                                        psum[:, src, :].rearrange("p (h d) -> p h d", h=4), ACT.Copy, scale=S1(s))
                        last.then_inc(sig("n6_ready"), 1)
                        act.wait_ge(sig("v6_ps_ready"), at(i, par, TT, t_ + 1))
                        nc.scalar.activation(v6[:, TT + t_, :], psum[:, 4, :], ACT.Copy, scale=S1("v6")).then_inc(sig("v6_ready"), 1)
                        nc.scalar.activation(v6[:, t_, :], psum[:, 5, :], ACT.Copy, scale=S1("vc6")).then_inc(sig("v6_ready"), 1)
                        act.wait_ge(sig("kT6_ps_ready"), at(i, par, TT, t_ + 1))
                        nc.scalar.activation(kT6[:, :, (TT + t_) * P:(TT + t_ + 1) * P], psum[:, 6, :].rearrange("p (g n) -> p g n", g=G3), ACT.Copy)
                        nc.scalar.activation(kT6[:, :, t_ * P:(t_ + 1) * P], psum[:, 7, :].rearrange("p (g n) -> p g n", g=G3),
                                             ACT.Copy).then_inc(sig("kT6_ready"), 1)
                    front_high(act, i, par + 1, 6, 1 - par)
                    for t_ in range(TT):
                        for n in range(4):
                            act.wait_ge(sig("q6_ps_ready"), at(i, par, 4 * TT, 4 * t_ + n + 1))
                            src = psum[:, 2 + n, :].rearrange("p (h d) -> p h d", h=4)
                            nc.scalar.activation(r6[:, 4 * n:4 * n + 4, :], src, ACT.Square, scale=S1("q6")).then_inc(sig("sq6_ready"), 1)
                            last = nc.scalar.activation(n6[:, 4 * n:4 * n + 4, :], src, ACT.Copy, scale=S1("q6"))
                        last.then_inc(sig("n6_ready"), 1)
                        for n in range(4):
                            act.wait_ge(sig("qT6_ps_ready"), at(i, par, 4 * TT, 4 * t_ + n + 1))
                            nc.scalar.activation(qT6[:, 4 * n:4 * n + 4, :], psum[:, 2 + n, :].rearrange("p (h q) -> p h q", h=4),
                                                 ACT.Copy).then_inc(sig("qT6_ready"), 1)
                        for h in range(H3):
                            u = t_ * H3 + h
                            nk = NK6[t_]
                            act.wait_ge(sig("nmax6_ready"), at(i, par, TT * H3, u + 1))
                            if h >= 2:
                                act.wait_ge(sig("pT6_ps_ready"), at(i, par, TT * H3, u - 1))
                            nc.scalar.activation(p6[:, h % 2, 0:nk], psum[:, 2 + h % 2, 0:nk], ACT.Exp, bias=nmax6[:, h % 2:h % 2 + 1],
                                                 scale=-1.0, accum_out=sum6[:, h:h + 1]).then_inc(sig("p6_ready"), 1)
                        for n in range(4):
                            act.wait_ge(sig("oT6_ps_ready"), at(i, par, 4 * TT, 4 * t_ + n + 1))
                            nc.scalar.activation(r6[:, 4 * n:4 * n + 4, :], psum[:, 2 + n, :].rearrange("p (h q) -> p h q", h=4),
                                                 ACT.Copy).then_inc(sig("oT6_ready"), 1)

        def dve_stage6(dve, dc):
            prep_dve(dve, dc, prep6, 6, HI6)
            dve.wait_ge(sig("tables_loaded"), 240)
            for wq in range(2):
                w = norm_w6[:, wq, :].unsqueeze(1)
                dc.step(nc.vector.tensor_tensor(rope6[:, wq, :, 0, :], rope6[:, wq, :, 0, :], w.broadcast_to([P, TT, P]), ALU.mult))
                for a, b in ((slice(0, 64), slice(64, P)), (slice(64, P), slice(0, 64))):
                    dc.step(nc.vector.tensor_tensor(rope6[:, wq, :, 1, a], rope6[:, wq, :, 1, a], w[:, :, b].broadcast_to([P, TT, 64]), ALU.mult))
            dc.step(nc.vector.tensor_copy(key_w6[:, :], norm_w6[:, 1, :]))
            dc.settle()
            dc.step(nc.vector.tensor_scalar(rope6[:, 0], rope6[:, 0], -SC6, None, ALU.mult))
            dc.step(nc.vector.tensor_scalar(tri6[:, :], tri_raw, -1.0, None, ALU.mult))
            for s, m in (("q6", "w3_q"), ("k6", "w3_k"), ("v6", "w3_v")):
                dc.step(nc.vector.tensor_scalar(S1(s), S1(f"inv_{m}"), 1.0 / LN_SCALE, None, ALU.mult))
            for s, m in (("kc6", "w3_kc"), ("vc6", "w3_vc")):
                dc.step(nc.vector.tensor_tensor(S1(s), S1(f"inv_{m}"), S1("inv_ctx"), ALU.mult))
            dve.wait_ge(sig("stage_free"), prep6[1][-1][0] + 1)
            dc.settle()
            nc.vector.tensor_copy(part[:, 30:31], S1("q6")).then_inc(sig("weights_ready"), 1)

            def rotate(i, par, r, n, wq, t_, extra):
                m = n + extra
                dve.wait_ge(sig("n6_ready"), at(i, par, NR6, r + 1))
                dc.link(nc.vector.reduce_sum(squares6[:, 0:m], r6[:, 0:m, :], AX.X))
                nc.vector.tensor_scalar(squares6[:, 0:m], squares6[:, 0:m], 1.0 / P, 1e-6, ALU.mult, ALU.add).then_inc(sig("squares6_ready"), 1)
                dc.step(nc.vector.tensor_tensor(r6[:, 0:n, :], n6[:, 0:n, :],
                                                rope6[:, wq, t_, 0, :].unsqueeze(1).broadcast_to([P, n, P]), ALU.mult))
                if extra:
                    dc.step(nc.vector.tensor_tensor(r6[:, n:m, :], n6[:, n:m, :], key_w6[:, :].unsqueeze(1).broadcast_to([P, extra, P]), ALU.mult))
                dve.wait_ge(sig("turn6_ready"), at(i, par, 2 * NR6, 2 * r + 2))
                dc.settle()
                dc.link(nc.vector.tensor_tensor(r6[:, 0:n, :], r6[:, 0:n, :], turn6[:, 0:n, :], ALU.add))
                dve.wait_ge(sig("root6_ready"), at(i, par, NR6, r + 1))
                nc.vector.tensor_tensor(r6[:, 0:m, :], r6[:, 0:m, :], root6[:, 0:m].unsqueeze(2).broadcast_to([P, m, P]),
                                        ALU.mult).then_inc(sig("r6_ready"), 1)

            with dve.Fori(0, PAIRS) as i:
                dc.enter(i, PER6, PAIRS)
                for par in range(2):
                    dve.wait_ge(sig("ctx6_high_ready"), at(i, par, 1, 1))
                    nc.vector.scalar_tensor_tensor(out=cl6, in0=cb6, scalar=S1("s_ctx"), in1=ch6, op0=ALU.mult,
                                                   op1=ALU.subtract).then_inc(sig("ctx6_low_ready"), 1)
                    for t_ in range(TT):
                        rotate(i, par, t_, G3, 1, t_, G3)
                    front_norm(dve, dc, i, par + 1, 6, following(i, par), 1 - par)
                    front_low(dve, i, par + 1, 6, 1 - par)
                    for t_ in range(TT):
                        rotate(i, par, TT + t_, H3, 0, t_, 0)
                        nk = NK6[t_]
                        for h in range(H3 + 1):
                            if h < H3:
                                u = t_ * H3 + h
                                dve.wait_ge(sig("s6_ready"), at(i, par, TT * H3, u + 1))
                                nc.vector.tensor_reduce(nmax6[:, h % 2:h % 2 + 1], psum[:, 2 + h % 2, 0:nk], AX.X,
                                                        ALU.min).then_inc(sig("nmax6_ready"), 1)
                            if h >= 1:
                                v = h - 1
                                u = t_ * H3 + v
                                dve.wait_ge(sig("pT6_ps_ready"), at(i, par, TT * H3, u + 1))
                                nc.vector.tensor_copy(pT6[:, v % 2, 0:nk // P, :], psum[:, 4 + v % 2, 0:nk].rearrange("p (n q) -> p n q", q=P)).then_inc(sig("pT6_ready"), 1)
                                if v % 4 == 3:
                                    q = v // 4
                                    dve.wait_ge(sig("p6_ready"), at(i, par, TT * H3, u + 1))
                                    dc.link(nc.vector.reciprocal(rsum6[:, 4 * q:4 * q + 4], sum6[:, 4 * q:4 * q + 4]))
                                    dve.wait_ge(sig("o6_ready"), at(i, par, 4 * TT, 4 * t_ + q + 1))
                                    nc.vector.tensor_tensor(n6[:, 4 * q:4 * q + 4, :], psum[:, 6 + q % 2, :].rearrange("p (h d) -> p h d", h=4),
                                                            rsum6[:, 4 * q:4 * q + 4].unsqueeze(2).broadcast_to([P, 4, P]),
                                                            ALU.mult).then_inc(sig("o6_drained"), 1)
                        xt = X[:, (i * 2 + par) * TT + t_, :]
                        dve.wait_ge(sig("y6_ready"), at(i, par, TT, t_ + 1))
                        nc.vector.scalar_tensor_tensor(out=xt, in0=psum[:, 1, :], scalar=gates[:, 3:4], in1=xt,
                                                       op0=ALU.mult, op1=ALU.add).then_inc(sig("x6_added"), 1)
                dc.leave()
            dve.wait_ge(sig("x6_added"), TT * B + 1)
            dve.sem_inc(sig("stage_done"), 1)

        HI6 = [0]
        PER6 = 48

        prep7 = add_prep(7, [("w3_up", 8, "sign", flat(area_a, 0, 8192), None), ("w3_down", 8, "sign", flat(area_a, 16384, 8192), None)])
        w7_up = view(area_a, 0, [KD, E], F16)
        w7_down = view(area_a, 16384, [KE, D], F16)
        up_scale = view(area_a, 32768, [KE])
        down_scale = view(area_a, 34816, [D])
        out_scale = view(area_a, 36864, [1])
        hTh7 = view(area_b, 0, [KE, S], F16)
        hTl7 = view(area_b, 8192, [KE, S], F16)
        hid7 = view(area_b, 16384, [2, 512])
        y7 = view(area_b, 20480, [TT, D])

        def sp_stage7(sp):
            sp.wait_ge(sig("stage_done"), 3)
            sp.dma_start(up_scale, t["up_scale"]).then_inc(sig("tables_loaded"), 16)
            sp.dma_start(down_scale, row("down_scale")).then_inc(sig("tables_loaded"), 16)
            sp.dma_start(out_scale, row("out_scale")).then_inc(sig("tables_loaded"), 16)
            prep_load(sp, prep7)
            sp.sem_inc(sig("hid7_ready"), 2 * 2)
            sp.sem_inc(sig("y7_drained"), TT)
            with sp.Fori(0, PAIRS) as i:
                for par in range(2):
                    sp.wait_ge(sig("x7_ready"), at(i, par, TT, TT))
                    xo = t["out"].rearrange("(b t p) d -> p b t d", p=P, t=TT)
                    sp.dma_start(xo[:, i * 2 + par], X[:, bass.ds((i * 2 + par) * TT, TT), :]).then_inc(sig("stored"), 16)
            sp.wait_ge(sig("stored"), 16 * B)

        def pool_stage7(pool, pc):
            pool.wait_ge(sig("bound_squares_ready"), 3)
            nc.gpsimd.tensor_tensor(part[:, 29:30], part[:, 28:29], half_pow[:, 0:1], ALU.pow).then_inc(sig("bound_roots_ready"), 1)
            with pool.Fori(0, PAIRS) as i:
                pc.enter(i, 2, PAIRS)
                for par in range(2):
                    front_rstd(pool, pc, i, par + 1, 7)
                pc.leave()

        def pe_stage7(pe):
            pe.wait_ge(sig("bound_sums_ready"), 4)
            nc.tensor.matmul(psum[:, 7, 0:1], ones[:, :], part[:, 24:25], start=True, stop=True).then_inc(sig("scale7_total_ready"), 1)
            pe.wait_ge(sig("weights_ready"), 4)

            def down(i, par, j):
                for t_ in range(TT):
                    if j == 0:
                        pe.wait_ge(sig("y7_drained"), at(i, par, TT, t_ + 1))
                    if t_ == 0:
                        pe.wait_ge(sig("hid7_low_ready"), at(i, par, NJ, j + 1))
                    for k in (2 * j, 2 * j + 1):
                        for n, h in enumerate((hTh7, hTl7)):
                            last = nc.tensor.matmul(psum[:, 6 + t_, :], h[:, k, t_ * P:(t_ + 1) * P], w7_down[:, k, :],
                                                    start=(k == 0 and n == 0), stop=(k == KE - 1 and n == 1))
                    if j == NJ - 1:
                        last.then_inc(sig("down7_ready"), 1)

            with pe.Fori(0, PAIRS) as i:
                for par in range(2):
                    front_done(pe, i, par, 7)
                    for j in range(NJ):
                        pe.wait_ge(sig("hid7_ready"), at(i, par, 2 * NJ, 2 * j + 2))
                        for m in (2 * j, 2 * j + 1):
                            out = psum[:, 2 + j % 2, (m % 2) * S:(m % 2 + 1) * S]
                            for k in range(KD):
                                for n, xt in enumerate((xTh, xTl)):
                                    last = nc.tensor.matmul(out, w7_up[:, k, m * P:(m + 1) * P], xt[:, par, k, :],
                                                            start=(k == 0 and n == 0), stop=(k == KD - 1 and n == 1))
                        last.then_inc(sig("up7_ready"), 1)
                        if j >= 2:
                            down(i, par, j - 2)
                        if j == 4:
                            front_transpose(pe, i, par + 1, 7, 1 - par)
                    down(i, par, NJ - 2)
                    down(i, par, NJ - 1)

        def act_stage7(act):
            act.wait_ge(sig("tables_loaded"), 288)
            nc.scalar.activation(part[:, 0:KE], up_scale, ACT.Square, accum_out=part[:, 24:25]).then_inc(sig("bound_sums_ready"), 1)
            prep_act(act, prep7, 7, None)
            act.wait_ge(sig("weights_ready"), 4)
            with act.Fori(0, PAIRS) as i:
                for par in range(2):
                    for j in range(NJ):
                        act.wait_ge(sig("up7_ready"), at(i, par, NJ, j + 1))
                        for m in range(2):
                            nc.scalar.activation(hid7[:, j % 2, m * S:(m + 1) * S], psum[:, 2 + j % 2, m * S:(m + 1) * S], ACT.Relu,
                                                 scale=up_scale[:, 2 * j + m:2 * j + m + 1]).then_inc(sig("hid7_ready"), 1)
                        if j == 4:
                            front_high(act, i, par + 1, 7, 1 - par)
                        act.wait_ge(sig("hid7_ready"), at(i, par, 2 * NJ, 2 * j + 6))
                        nc.scalar.activation(hTh7[:, 2 * j:2 * j + 2, :], hid7[:, j % 2, :].rearrange("p (m s) -> p m s", m=2),
                                             ACT.Copy).then_inc(sig("hid7_high_ready"), 1)
                        if j >= 1:
                            act.wait_ge(sig("hid7_low_ready"), at(i, par, NJ, j))

        def dve_stage7(dve, dc):
            dve.wait_ge(sig("tables_loaded"), 288)
            dve.wait_ge(sig("scale7_total_ready"), 1)
            nc.vector.tensor_scalar(part[:, 28:29], psum[:, 7, 0:1], 1e-30, None, ALU.max).then_inc(sig("bound_squares_ready"), 1)
            dve.wait_ge(sig("bound_roots_ready"), 3)
            dc.step(nc.vector.tensor_scalar(up_scale, up_scale, part[:, 29:30], 2.0 ** 6 / LN_SCALE, ALU.mult, ALU.mult))
            dc.step(nc.vector.scalar_tensor_tensor(out=part[:, 30:31], in0=part[:, 28:29], scalar=2.0 ** -6, in1=part[:, 29:30],
                                                   op0=ALU.mult, op1=ALU.mult))
            dc.settle()
            dc.link(nc.vector.tensor_tensor(part[:, 30:31], part[:, 30:31], gates[:, 7:8], ALU.mult))
            dc.link(nc.vector.tensor_tensor(S1("y7"), part[:, 30:31], out_scale, ALU.mult))
            dc.link(nc.vector.tensor_scalar(down_scale, down_scale, S1("y7"), None, ALU.mult))
            dve.wait_ge(sig("stage_free"), prep7[1][-1][0] + 1)
            nc.vector.tensor_copy(part[:, 30:31], S1("y7")).then_inc(sig("weights_ready"), 1)
            with dve.Fori(0, PAIRS) as i:
                dc.enter(i, 4, PAIRS)
                for par in range(2):
                    front_norm(dve, dc, i, par + 1, 7, following(i, par), 1 - par)
                    for j in range(NJ):
                        if j == 4:
                            front_low(dve, i, par + 1, 7, 1 - par)
                        dve.wait_ge(sig("hid7_high_ready"), at(i, par, NJ, j + 1))
                        nc.vector.tensor_tensor(hTl7[:, 2 * j:2 * j + 2, :], hid7[:, j % 2, :].rearrange("p (m s) -> p m s", m=2),
                                                hTh7[:, 2 * j:2 * j + 2, :], ALU.subtract).then_inc(sig("hid7_low_ready"), 1)
                    for t_ in range(TT):
                        dve.wait_ge(sig("down7_ready"), at(i, par, TT, t_ + 1))
                        nc.vector.tensor_tensor(y7[:, t_, :], psum[:, 6 + t_, :], down_scale, ALU.mult).then_inc(sig("y7_drained"), 1)
                    dve.wait_ge(sig("y7_drained"), at(i, par, TT, 2 * TT))
                    for t_ in range(TT):
                        xt = X[:, (i * 2 + par) * TT + t_, :]
                        nc.vector.tensor_tensor(xt, xt, y7[:, t_, :], ALU.add).then_inc(sig("x7_ready"), 1)
                dc.leave()

        SP_STAGES = [sp_stage0, sp_stage1, sp_stage2, sp_stage3, sp_stage4, sp_stage5, sp_stage6, sp_stage7]
        POOL_STAGES = [pool_stage0, pool_stage1, pool_stage2, pool_stage3, pool_stage4, pool_stage5, pool_stage6, pool_stage7]
        ACT_STAGES = [act_stage0, act_stage1, act_stage2, act_stage3, act_stage4, act_stage5, act_stage6, act_stage7]
        DVE_STAGES = [dve_stage0, dve_stage1, dve_stage2, dve_stage3, dve_stage4, dve_stage5, dve_stage6, dve_stage7]
        PE_STAGES = [pe_stage0, pe_stage1, pe_stage2, pe_stage3, pe_stage4, pe_stage5, pe_stage6, pe_stage7]

        @block.sync
        def _(sp):
            sp_constants(sp)
            for stage_program in SP_STAGES:
                stage_program(sp)

        @block.gpsimd
        def _(pool):
            pc = Chain(pool, sig("pool_steps"))
            pc.link(nc.gpsimd.memset(half_pow[:, :], -0.5))
            pc.link(nc.gpsimd.memset(eps_col[:, :], LN_EPS))
            for stage_program in POOL_STAGES:
                stage_program(pool, pc)

        @block.scalar
        def _(act):
            for stage_program in ACT_STAGES:
                stage_program(act)

        @block.vector
        def _(dve):
            dc = Chain(dve, sig("dve_steps"))
            for stage_program in DVE_STAGES:
                stage_program(dve, dc)

        @block.tensor
        def _(pe):
            for stage_program in PE_STAGES:
                stage_program(pe)


def rope_table():
    inv = (1.0 / np.float32(10000.0) ** (np.arange(0, 128, 2, dtype=np.float32) / np.float32(128))).astype(np.float32)
    ang = np.outer(np.arange(S, dtype=np.float32), inv).astype(np.float32)
    ang = np.concatenate([ang, ang], -1)
    sign = np.concatenate([-np.ones(64, np.float32), np.ones(64, np.float32)])
    tab = np.stack([np.cos(ang), np.sin(ang) * sign], 1).astype(np.float32)
    return np.ascontiguousarray(tab.reshape(TT, P, 2, P).transpose(1, 0, 2, 3))


def kernel(**inputs):
    import concourse.bacc as bacc
    from concourse.bass_utils import run_bass_kernel_spmd

    a = {k: np.asarray(v) for k, v in inputs.items()}

    def packed(w):
        return np.ascontiguousarray(w.reshape(-1, P, w.shape[1]).transpose(1, 0, 2).reshape(P, -1))

    q = np.arange(P)
    ctx = a["ctx_2048"]
    kpad = np.zeros((HC, P - 1 + D), np.float32)
    kpad[:, P - 1:] = a["L0_xattn_k"]
    toeplitz = np.ascontiguousarray(np.lib.stride_tricks.sliding_window_view(kpad, D, axis=1)[:, ::-1])
    arrays = {
        "x": a["x"].reshape(-1, D),
        "ctx": ctx.reshape(-1, D),
        "ctxT": np.ascontiguousarray(ctx.reshape(B, S, KD, P).transpose(3, 2, 0, 1)),
        "toeplitz": toeplitz,
        "skip": np.ascontiguousarray(a["fside_S2_0"].reshape(TT, P).T),
        "gates": np.concatenate([a["g_xattn"], a["g_ffn"]]),
        "c_ident": np.eye(P, dtype=np.float32),
        "c_block": (q[:, None] // HW == q[None, :] // HW).astype(np.float32),
        "c_tri": np.where(q[None, :] > q[:, None], np.float32(NEG), np.float32(0)),
        "c_rope": rope_table(),
        "w0_up": packed(a["L0_ffn_W_up"].T), "w0_gate": packed(a["L0_ffn_W_gate"].T), "w0_down": packed(a["L0_ffn_W_down"].T),
        "wkv_w": np.ascontiguousarray(a["L1_xattn_w"].reshape(KD, P).T), "wkv_u": np.ascontiguousarray(a["L1_xattn_u"].reshape(KD, P).T),
        "w1": packed(a["L1_ffn_weight"].T), "w1_scale": a["L1_ffn_scale_weight"], "w1_bias": a["L1_ffn_bias"],
        "w2_q": packed(a["L2_xattn_Wq"].T),
        "w2_kv": packed(np.concatenate([a["L2_xattn_Wk"], a["L2_xattn_Wv"]], 0).T), "w2_o": packed(a["L2_xattn_Wo"].T),
        "b2_q": a["L2_xattn_bq"], "b2_kv": np.concatenate([a["L2_xattn_bk"], a["L2_xattn_bv"]]), "b2_o": a["L2_xattn_bo"],
        "mask_q": a["mask_SxS2_bc0"], "mask_b": a["mask_BxS2_bk0"],
        "w2_syn": packed(a["L2_ffn_W_syn"].T), "w2_out": packed(a["L2_ffn_W_out"].T), "b2_syn": a["L2_ffn_b_syn"],
        "b2_out": a["L2_ffn_b_out"], "gamma": a["L2_ffn_gamma"], "beta": a["L2_ffn_beta"],
        "w3_q": packed(a["L3_xattn_wq"]), "w3_k": packed(a["L3_xattn_wk"]), "w3_v": packed(a["L3_xattn_wv"]),
        "w3_kc": packed(a["L3_xattn_wk_ctx"]), "w3_vc": packed(a["L3_xattn_wv_ctx"]), "w3_o": packed(a["L3_xattn_wo"]),
        "qn_w": a["L3_xattn_q_norm_w"], "kn_w": a["L3_xattn_k_norm_w"],
        "w3_up": packed(a["L3_ffn_up_weight"].T), "w3_down": packed(a["L3_ffn_down_weight"].T),
        "up_scale": np.ascontiguousarray(a["L3_ffn_up_scale"].reshape(KE, P).T), "down_scale": a["L3_ffn_down_scale"],
        "out_scale": a["L3_ffn_output_scale"],
    }
    nc = bacc.Bacc("TRN2", target_bir_lowering=False, num_devices=1)
    t, given = {}, {}
    for name, v in arrays.items():
        given[f"in_{name}"] = v
        t[name] = nc.dram_tensor(f"in_{name}", v.shape, mybir.dt.from_np(v.dtype), kind="ExternalInput").ap()
    t["out"] = nc.dram_tensor("out_x", (B * S, D), F32, kind="ExternalOutput").ap()
    build(nc, t)
    r = run_bass_kernel_spmd(nc, [given], core_ids=[0])
    return r.results[0]["out_x"].reshape(B, S, D)
```
